# Optimizing a Trainium2 kernel written in Bass

```python
import numpy as np
import jax
import jax.numpy as jnp

def _softmax(x, axis=-1):
    return jax.nn.softmax(x, axis=axis)

def _gelu(x):
    return jax.nn.gelu(x, approximate=True)

def _silu(x):
    return jax.nn.silu(x)

def _sigmoid(x):
    return jax.nn.sigmoid(x)

def _layernorm(x, axis=-1, eps=1e-05):
    m = jnp.mean(x, axis=axis, keepdims=True)
    v = jnp.var(x, axis=axis, keepdims=True)
    return (x - m) / jnp.sqrt(v + eps)

def _scatter_add(tgt, idx, src, axis=0):
    return tgt.at[idx].add(src)

def _segment_sum(src, seg, n):
    return jax.ops.segment_sum(src, seg, n)
kernel_name = 'mk_adaln_d1_jaxref_r4_ee8f5a'

def setup_inputs(seed: int=0):
    np.random.seed(seed)
    _w = jnp.asarray

    def _L0_attn_setup():
        import jax, jax.numpy as jnp
        import numpy as np
        DIM = 256
        HEADS = 16
        HEAD_DIM = DIM // HEADS
        SCALE = float(HEAD_DIM ** (-0.25))
        ROPE_BASE = 10000.0

        def apply_rope(x):
            B, N, H, D = x.shape
            half = D // 2
            inv_freq = 1.0 / ROPE_BASE ** (jnp.arange(half, dtype=jnp.float32) / half)
            freqs = jnp.arange(N, dtype=jnp.float32)[:, None] * inv_freq[None, :]
            cos = jnp.cos(freqs)[None, :, None, :].astype(x.dtype)
            sin = jnp.sin(freqs)[None, :, None, :].astype(x.dtype)
            x1, x2 = (x[..., :half], x[..., half:])
            return jnp.concatenate([x1 * cos - x2 * sin, x1 * sin + x2 * cos], axis=-1)
        key = jax.random.key(seed)
        k1, k2, k3 = jax.random.split(key, 3)
        x = jax.random.normal(k1, (4, 1024, DIM), dtype=jnp.float32)
        w_qkv = jax.random.normal(k2, (DIM, 3 * DIM), dtype=jnp.float32) * 0.02
        w_out = jax.random.normal(k3, (DIM, DIM), dtype=jnp.float32) * 0.02
        return {'x': x, 'w_qkv': w_qkv, 'w_out': w_out}
    _L0_attn_in = _L0_attn_setup()

    def _L0_ffn_setup():
        import jax, jax.numpy as jnp
        import numpy as np
        B, S, D, H, E = (2, 512, 256, 1024, 8)
        key = jax.random.key(seed)
        k0, k1, k2, k3 = jax.random.split(key, 4)
        x = jax.random.normal(k0, (B, S, D), dtype=jnp.float32)
        router_w = jax.random.normal(k1, (E, D), dtype=jnp.float32) * 0.02
        w1 = jax.random.normal(k2, (E, D, H), dtype=jnp.float32) * 0.02
        w2 = jax.random.normal(k3, (E, H, D), dtype=jnp.float32) * 0.02
        return {'x': x, 'router_w': router_w, 'w1': w1, 'w2': w2}
    _L0_ffn_in = _L0_ffn_setup()
    _L0_c = _w((lambda *s: np.random.randn(*s).astype(np.float32) * 0.05)(8, 256))
    _L0_wmod = _w((lambda *s: np.random.randn(*s).astype(np.float32) * 0.05)(256, 6 * 256) * 256 ** (-0.5))
    _d = {'L0_attn_x': _L0_attn_in['x'], 'L0_attn_w_qkv': _L0_attn_in['w_qkv'], 'L0_attn_w_out': _L0_attn_in['w_out'], 'L0_ffn_router_w': _L0_ffn_in['router_w'], 'L0_ffn_w1': _L0_ffn_in['w1'], 'L0_ffn_w2': _L0_ffn_in['w2'], 'L0_c': _L0_c, 'L0_wmod': _L0_wmod}
    _x0 = _d['L0_attn_x']
    _d['L0_attn_x'] = jax.random.normal(jax.random.fold_in(jax.random.key(seed), 1), (8, 512, 256), dtype=_x0.dtype)
    del _x0
    return _d

def reference(L0_attn_x, L0_attn_w_qkv, L0_attn_w_out, L0_ffn_router_w, L0_ffn_w1, L0_ffn_w2, L0_c, L0_wmod):

    def _L0_attn_ref(x, w_qkv, w_out):
        import jax, jax.numpy as jnp
        import numpy as np
        DIM = 256
        HEADS = 16
        HEAD_DIM = DIM // HEADS
        SCALE = float(HEAD_DIM ** (-0.25))
        ROPE_BASE = 10000.0

        def apply_rope(x):
            B, N, H, D = x.shape
            half = D // 2
            inv_freq = 1.0 / ROPE_BASE ** (jnp.arange(half, dtype=jnp.float32) / half)
            freqs = jnp.arange(N, dtype=jnp.float32)[:, None] * inv_freq[None, :]
            cos = jnp.cos(freqs)[None, :, None, :].astype(x.dtype)
            sin = jnp.sin(freqs)[None, :, None, :].astype(x.dtype)
            x1, x2 = (x[..., :half], x[..., half:])
            return jnp.concatenate([x1 * cos - x2 * sin, x1 * sin + x2 * cos], axis=-1)
        B, N, D = x.shape
        qkv = x @ w_qkv
        q, k, v = jnp.split(qkv, 3, axis=-1)
        q = q.reshape(B, N, HEADS, HEAD_DIM)
        k = k.reshape(B, N, HEADS, HEAD_DIM)
        v = v.reshape(B, N, HEADS, HEAD_DIM)
        q = apply_rope(q)
        k = apply_rope(k)
        q = jax.nn.elu(q * SCALE) + 1.0
        k = jax.nn.elu(k * SCALE) + 1.0
        qT = jnp.moveaxis(q, 1, 0)
        kT = jnp.moveaxis(k, 1, 0)
        vT = jnp.moveaxis(v, 1, 0)
        kv0 = jnp.zeros((B, HEADS, HEAD_DIM, HEAD_DIM), dtype=q.dtype)
        ks0 = jnp.zeros((B, HEADS, HEAD_DIM), dtype=q.dtype)

        def step(carry, qkv_t):
            kv, ks = carry
            qt, kt, vt = qkv_t
            kv = kv + jnp.einsum('bhd,bhm->bhdm', kt, vt)
            ks = ks + kt
            denom = jnp.maximum(jnp.einsum('bhd,bhd->bh', qt, ks), 1e-06)
            out_t = jnp.einsum('bhd,bhdm->bhm', qt, kv) / denom[..., None]
            return ((kv, ks), out_t)
        _, outT = jax.lax.scan(step, (kv0, ks0), (qT, kT, vT))
        out = jnp.moveaxis(outT, 0, 1).reshape(B, N, D)
        return out @ w_out

    def _L0_ffn_ref(x, router_w, w1, w2):
        import jax, jax.numpy as jnp
        import numpy as np
        B, S, D, H, E = (2, 512, 256, 1024, 8)
        b, s, d = x.shape
        e = router_w.shape[0]
        xf = x.reshape(-1, d)
        probs = jax.nn.softmax(xf @ router_w.T, axis=-1)
        topv, topi = jax.lax.top_k(probs, 2)
        topv = topv / (topv.sum(axis=-1, keepdims=True) + 1e-09)
        cw = (jax.nn.one_hot(topi, e, dtype=xf.dtype) * topv[..., None]).sum(axis=1)
        h = jax.nn.gelu(jnp.einsum('td,edh->teh', xf, w1), approximate=False)
        y = jnp.einsum('teh,ehd->ted', h, w2)
        out = jnp.einsum('te,ted->td', cw, y)
        return out.reshape(b, s, d)
    x = L0_attn_x
    mod = (_silu(L0_c) @ L0_wmod).reshape(L0_c.shape[0], 6, 1, -1)
    sa, ca, ga, sb, cb, gb = (mod[:, 0], mod[:, 1], mod[:, 2], mod[:, 3], mod[:, 4], mod[:, 5])
    ga = (2 * (ga >= 0) - 1) * jnp.maximum(jnp.abs(ga), 0.25)
    gb = (2 * (gb >= 0) - 1) * jnp.maximum(jnp.abs(gb), 0.25)
    h = _layernorm(x, axis=-1) * (1 + ca) + sa
    x = x + ga * _L0_attn_ref(h, L0_attn_w_qkv, L0_attn_w_out)
    h = _layernorm(x, axis=-1) * (1 + cb) + sb
    x = x + gb * _L0_ffn_ref(h, L0_ffn_router_w, L0_ffn_w1, L0_ffn_w2)
    return x

_drawn_inputs = setup_inputs


def setup_inputs(seed=0):
    import zlib

    import numpy as np

    out = dict(_drawn_inputs(seed))
    spreads = {}
    factors = {'L0_attn_w_qkv': 8.0,
     'L0_attn_w_out': 8.0,
     'L0_ffn_router_w': 3.299,
     'L0_ffn_w1': 2.946,
     'L0_ffn_w2': 2.867,
     'L0_c': 2.839,
     'L0_wmod': 2.832}
    for name, (base, spread) in spreads.items():
        noise = np.random.default_rng([zlib.crc32(name.encode()), seed]).standard_normal(out[name].shape)
        drawn = base * np.exp(spread * noise) if base else spread * noise
        out[name] = jnp.asarray(drawn.astype(out[name].dtype))
    for name, factor in factors.items():
        out[name] = (out[name] * factor).astype(out[name].dtype)
    return out
```

```python
from contextlib import ExitStack

import numpy as np

import concourse.bass as bass
from concourse import mybir

ALU = mybir.AluOpType
ACT = mybir.ActivationFunctionType
AX_X = mybir.AxisListType.X
F32 = mybir.dt.float32
F16 = mybir.dt.float16
I32 = mybir.dt.int32
U32 = mybir.dt.uint32

P = 128
B, S, D = 8, 512, 256
NH, HD = 16, 16
E, H = 8, 1024
KT = D // P
MT = H // P
CPB = S // P
NC = B * CPB
T = B * S
VW = HD + 1
HG = 8
EW = KT * H
PIECE = 2 * EW // CPB
MAXB = (2 * T + E * (P - 1)) // P
TB = MAXB + MAXB % 2
LN_EPS = 1e-5
DEN_MIN = 1e-6
TOP_EPS = 1e-9
GATE_MIN = 0.25
WS = 64.0
Q_SCALE = float(HD ** -0.25)
LAG_A = 4
LAG_C = 2
NOWHERE = 2 * T
UC = 4


class At:

    def __init__(self, b, c, unroll):
        self.unroll, self.b, self.c = unroll, b + c // unroll, c % unroll
        self.n = self.b * unroll + self.c
        self.p = self.c % 2
        self.pairs = self.b * (unroll // 2) + self.c // 2

    def back(self, k):
        return At(self.b, self.c - k, self.unroll)

    def inside(self, count):
        return not isinstance(self.n, int) or 0 <= self.n < count


def wait(eng, sem, value, most=None):
    if isinstance(value, int):
        if most is not None:
            value = min(value, most)
        if value <= 0:
            return
    eng.wait_ge(sem, value)


def adaln_block(nc, x, w_qkv, w_out, router_w, w1, w2, c_in, wmod, rope_cos, rope_sin, out):
    ctx = ExitStack()
    with ctx:
        def sb(name, shape, dt=F32):
            return ctx.enter_context(nc.sbuf_tensor(name, shape, dt))

        def sem(name):
            return ctx.enter_context(nc.semaphore(name))

        bank = [ctx.enter_context(nc.psum_tensor(f"bank{i}", [P, 512], F32)) for i in range(8)]
        mod_d = nc.dram_tensor("mod_rows", (B, 6 * D), F32, kind="Internal").ap()
        rows_d = nc.dram_tensor("ffn_rows", (T, 2 * D), F32, kind="Internal").ap()

        w1hi = sb("w1hi", [P, E * EW], F16)
        w1lo = sb("w1lo", [P, E * EW], F16)
        w2hi = sb("w2hi", [P, E * EW], F16)
        w2lo = sb("w2lo", [P, E * EW], F16)
        stage = sb("stage", [P, 2, PIECE])

        ident = sb("ident", [P, P])
        ident16 = sb("ident16", [P, P], F16)
        causal = sb("causal", [P, P])
        before = sb("before", [P, P])
        ones = sb("ones", [P, P])
        headmask = sb("headmask", [P, HG, VW])
        cos_t = sb("cos_t", [P, CPB, HD // 2])
        sin_t = sb("sin_t", [P, CPB, 2, HD // 2])
        wqhi = sb("wqhi", [P, KT, 3 * D], F16)
        wqlo = sb("wqlo", [P, KT, 3 * D], F16)
        wohi = sb("wohi", [P, KT, D], F16)
        wolo = sb("wolo", [P, KT, D], F16)
        rwT = sb("rwT", [P, KT, E])
        mod_a = sb("mod_a", [P, 2 * D])
        mod_b = sb("mod_b", [P, 4 * D])
        logits = sb("logits", [P, E, NC])

        xt = sb("xt", [P, 2 * CPB * D])
        st = sb("st", [P, 2, 6])
        mv = sb("mv", [P, 2, 2])
        var = sb("var", [P, 2])
        rstd = sb("rstd", [P, 2])
        eps = sb("eps", [P, 1])
        minus_half = sb("minus_half", [P, 1])
        xn = sb("xn", [P, 2, D])
        hThi = sb("hThi", [P, D], F16)
        hTlo = sb("hTlo", [P, D], F16)
        ra = sb("ra", [P, 2 * D])
        rb = sb("rb", [P, 2 * D])
        expo = sb("expo", [P, 2 * D])
        feat = sb("feat", [P, 2, 2 * D])
        vx = sb("vx", [P, 2, NH, VW])
        qst = sb("qst", [P, NH, 4, HD], F16)
        kst = sb("kst", [P, NH, 4, HD], F16)
        qstT = sb("qstT", [P, 8 * P], F16)
        kstT = sb("kstT", [P, 8 * P], F16)
        qT = sb("qT", [P, D])
        am = sb("am", [P, 2, 2, 4 * P])
        state = sb("state", [P, 2, 2 * HG * VW])
        state_add = sb("state_add", [P, 2 * HG * VW])
        den = sb("den", [P, 2, NH])
        attn = sb("attn", [P, D])
        aThi = sb("aThi", [P, D], F16)
        aTlo = sb("aTlo", [P, D], F16)
        x1 = sb("x1", [P, 2, D])
        h2 = sb("h2", [P, 2, D])
        h2T = sb("h2T", [P, D])

        iota_i = sb("iota_i", [P, P], I32)
        iota_f = sb("iota_f", [P, P])
        tile_i = sb("tile_i", [P, NC], I32)
        tile_f = sb("tile_f", [P, NC])
        id1 = sb("id1", [P, NC])
        small = expo[:, 0:14 * NC].rearrange("p (k i) -> p k i", k=14)
        slot_i = ra[:, 0:4 * NC].bitcast(I32).rearrange("p (u k i) -> p u k i", u=2, k=2)
        slot_f = ra[:, 4 * NC:8 * NC].rearrange("p (u k i) -> p u k i", u=2, k=2)
        block_e = sb("block_e", [P, TB], I32)
        gidx = sb("gidx", [P, TB], I32)
        sidx = sb("sidx", [P, TB], I32)
        cwT = sb("cwT", [P, TB])
        gi = sb("gi", [P, UC], U32)
        si = sb("si", [P, UC], U32)

        xg = xt[:, :].rearrange("p (q n) -> p q n", q=UC)
        g32 = am[:, :, :, :].rearrange("p g o n -> p g (o n)")
        def halves(t):
            return t.rearrange("p (q n) -> p q n", q=2)
        ghi = halves(feat[:, :, :].rearrange("p q n -> p (q n)").bitcast(F16))
        glo = halves(mod_b[:, :].bitcast(F16))
        xghi = halves(qstT[:, 0:2 * D])
        xglo = halves(kstT[:, 0:2 * D])
        yw = x1
        b_rhs = qst[:, :, :, :].rearrange("p h c d -> p (h c d)").bitcast(F32)[:, 0:4 * TB].rearrange(
            "p (k q j) -> p k q j", k=2, q=2)
        b_one = kst[:, :, :, :].rearrange("p h c d -> p (h c d)").bitcast(F32)[:, 0:2 * P].rearrange(
            "p (k t) -> p k t", k=2)
        w_ones = rb[:, 0:E * NC]
        rev = sb("rev", [P, E])

        half = E // 2 * EW
        late = [t[:, half:2 * half].bitcast(F32) for t in (w2hi, w2lo, w1lo)]
        wmod_raw = late[0][:, 0:KT * 6 * D].rearrange("p (k n) -> p k n", k=KT)
        wq_raw = late[1][:, 0:KT * 3 * D].rearrange("p (k n) -> p k n", k=KT)
        wo_raw = late[1][:, 1536:1536 + KT * D].rearrange("p (k n) -> p k n", k=KT)
        rw_raw = late[1][0:E, 2048:2048 + D]
        c_raw = late[1][0:B, 2304:2304 + D]
        c_exp = late[1][0:B, 2560:2560 + D]
        c_silu = late[1][0:B, 2816:2816 + D]
        cT = late[1][:, 3072:3072 + KT * B].rearrange("p (k b) -> p k b", k=KT)
        mod_s = late[2][0:B, 0:6 * D]
        gate_s = late[2][0:B, 1536:1536 + D]
        gate_a = late[2][0:B, 1792:1792 + D]

        def counters(prefix, names):
            return {k: sem(prefix + k) for k in names.split()}

        a_ = counters("a_", "st mv ve rs xn hm h hT hhi hlo qkv v rope R exp f shi slo Tq T qTs kTs qTf sc0 m0"
                            " sc1 m1 pv0 pv1 state stt stm stm0 den rec at aT ahi alo pj t1 x1 st2 mv2 ve2"
                            " rs2 xn2 hm2 h2 h2T h2e lg lge whi wsc wlo")
        s_x = [sem(f"s_x{c}") for c in range(CPB)]
        s_moda = sem("s_moda")
        s_modb = sem("s_modb")
        s_w = [sem("s_w0"), sem("s_w1")]
        s_out = [sem("s_out0"), sem("s_out1")]
        s_row = [sem("s_row0"), sem("s_row1")]
        s_ld = {k: sem("s_ld_" + k) for k in ("c", "wmod", "wq", "wo", "rw", "cos", "sin")}
        s_pool = sem("s_pool")
        s_dve = sem("s_dve")
        s_pe = sem("s_pe")
        s_act = sem("s_act")
        s_ms = sem("s_ms")
        b_ = counters("b_", "a mm")
        s_carry = sem("s_carry")
        c_ = counters("c_", "gi xT xhi xlo hA hB gA gB glA glB y yw")
        s_g = [sem(f"s_g{q}") for q in range(UC)]
        s_sc = sem("s_sc")

        x_rows = x.rearrange("b s d -> (b s) d")
        out_rows = out.rearrange("b s d -> (b s) d")
        w1_v = w1.rearrange("e (k p) h -> p e k h", p=P)
        w2_v = w2.rearrange("e (m p) d -> p e m d", p=P)
        MOD = {k: i * D for i, k in enumerate(("sa", "ca", "ga", "sb", "cb", "gb"))}

        def mod_row(k):
            return mod_a[:, MOD[k]:MOD[k] + D] if MOD[k] < 2 * D else mod_b[:, MOD[k] - 2 * D:MOD[k] - D]

        def x_slot(a):
            return xt[:, bass.ds((a.b % 2) * (CPB * D) + a.c * D, D)]

        def steps_a(eng, step):
            for c in range(CPB):
                step(At(0, c, CPB))
            with eng.Fori(1, B - 1) as b:
                for c in range(CPB):
                    step(At(b, c, CPB))
            for c in range(CPB + LAG_A):
                step(At(B - 1, c, CPB))

        def steps_c(eng, step):
            for c in range(UC):
                step(At(0, c, UC))
            with eng.Fori(1, MAXB // UC) as b:
                for c in range(UC):
                    step(At(b, c, UC))
            for c in range(MAXB % UC + LAG_C):
                step(At(MAXB // UC, c, UC))

        class Chain:

            def __init__(self, eng, sem_):
                self.eng, self.sem, self.n = eng, sem_, 0

            def __call__(self, ins):
                self.n += 1
                ins.then_inc(self.sem, 1)
                self.eng.wait_ge(self.sem, self.n)

        def piece(a, part):
            t = (w1hi, w1lo, w2hi, w2lo)[2 * (a.c // KT) + part]
            return t[:, bass.ds(a.b * EW + (a.c % KT) * PIECE, PIECE)]

        block = ctx.enter_context(nc.Block())

        marks = {}

        def carry(eng):
            eng.sem_inc(s_carry, 1)

        POOL_CONST = 15
        ACT_EXP, ACT_W, ACT_EXP2 = 1, 3, 4
        PE_T, PE_MOD, PE_RANK, PE_TABLE = 1, 2, 3, 4

        @block.vector
        def _(dve):
            link = Chain(dve, s_dve)
            v = nc.vector

            dve.wait_ge(s_act, ACT_EXP)
            link(v.tensor_scalar(c_exp, c_exp, 1.0, None, ALU.add))
            link(v.reciprocal(c_exp, c_exp))
            link(v.tensor_tensor(c_silu, c_raw, c_exp, ALU.mult))
            marks["silu"] = link.n
            dve.wait_ge(s_pe, PE_T)
            link(v.tensor_copy(cT, bank[0][:, 0:KT * B].rearrange("p (k b) -> p k b", k=KT)))
            link(v.tensor_copy(rwT[:, :, :], bank[0][:, KT * B:KT * (B + E)].rearrange("p (k e) -> p k e", k=KT)))
            marks["t"] = link.n
            dve.wait_ge(s_pe, PE_MOD)
            for k, add in (("sa", 0.0), ("ca", 1.0), ("ga", None), ("sb", 0.0), ("cb", 1.0), ("gb", None)):
                o = MOD[k]
                src, dst = bank[1 + o // 512][0:B, o % 512:o % 512 + D], mod_s[:, o:o + D]
                if add is None:
                    link(v.tensor_scalar(gate_s, src, 0.0, 2.0, ALU.is_ge, ALU.mult))
                    link(v.tensor_copy(gate_a, src))
                    link(v.scalar_tensor_tensor(out=gate_a, in0=gate_a, scalar=-1.0, in1=gate_a,
                                                op0=ALU.mult, op1=ALU.max))
                    link(v.tensor_scalar(gate_a, gate_a, GATE_MIN, None, ALU.max))
                    link(v.scalar_tensor_tensor(out=dst, in0=gate_s, scalar=-1.0, in1=gate_a,
                                                op0=ALU.add, op1=ALU.mult))
                else:
                    link(v.tensor_scalar(dst, src, add, None, ALU.add))
            marks["mod"] = link.n
            dve.wait_ge(s_act, ACT_W)
            for raw, hi, lo in ((wq_raw, wqhi, wqlo), (wo_raw, wohi, wolo)):
                link(v.scalar_tensor_tensor(out=lo[:, :, :], in0=raw, scalar=WS, in1=hi[:, :, :],
                                            op0=ALU.mult, op1=ALU.subtract))
            marks["wo"] = link.n
            dve.wait_ge(s_pool, POOL_CONST)
            dve.wait_ge(s_ld["cos"], 16)
            dve.wait_ge(s_ld["sin"], 16)

            def moments(src, k, done_stats, done, count):
                v.bn_stats(st[:, k, :], src).then_inc(done_stats, 1)
                wait(dve, done_stats, count)
                carry(dve)
                v.bn_aggr(mv[:, k, :], st[:, k, :]).then_inc(done, 1)

            def normalise(src, k, dst, rs, done, count):
                wait(dve, rs, count)
                v.tensor_scalar(dst, src, mv[:, k, 0:1], rstd[:, k:k + 1], ALU.subtract, ALU.mult)\
                    .then_inc(done, 1)

            def step(a):
                m = a.back(1)
                if m.inside(NC):
                    wait(dve, a_["hhi"], m.n + 1)
                    wait(dve, a_["qkv"], m.n)
                    v.tensor_tensor(hTlo[:, :], bank[0][:, 0:D], hThi[:, :], ALU.subtract)\
                        .then_inc(a_["hlo"], 1)
                m = a.back(2)
                if m.inside(NC):
                    wait(dve, a_["Tq"], m.n + 1)
                    wait(dve, a_["sc1"], m.n)
                    v.tensor_copy(qstT[:, :], bank[3][:, :].bitcast(F16)).then_inc(a_["qTs"], 1)
                m = a.back(3)
                if m.inside(NC):
                    wait(dve, a_["ahi"], m.n + 1)
                    wait(dve, a_["pj"], m.n)
                    v.tensor_tensor(aTlo[:, :], bank[7][:, 0:D], aThi[:, :], ALU.subtract)\
                        .then_inc(a_["alo"], 1)
                m = a.back(1)
                if m.inside(NC):
                    wait(dve, a_["qkv"], m.n + 1)
                    half_d = HD // 2
                    qk = bank[1][:, :].rearrange("p (h o d) -> p h o d", o=2, d=half_d)
                    rbv = rb[:, :].rearrange("p (h o d) -> p h o d", o=2, d=half_d)
                    v.tensor_tensor(ra[:, :].rearrange("p (h d) -> p h d", d=half_d),
                                    bank[1][:, :].rearrange("p (h d) -> p h d", d=half_d),
                                    cos_t[:, m.c:m.c + 1, :].broadcast_to([P, 4 * NH, half_d]), ALU.mult)
                    for o in range(2):
                        last = v.tensor_tensor(rbv[:, :, o, :], qk[:, :, 1 - o, :],
                                               sin_t[:, m.c, o:o + 1, :].broadcast_to([P, 2 * NH, half_d]),
                                               ALU.mult)
                    last.then_inc(a_["rope"], 1)
                m = a.back(2)
                if m.inside(NC):
                    wait(dve, a_["sc0"], m.n + 1)
                    wait(dve, a_["pv0"], m.n)
                    mask(0, "m0")
                m = a.back(3)
                if m.inside(NC):
                    wait(dve, a_["pj"], m.n + 1)
                    wait(dve, s_out[m.p], 16 * m.pairs)
                    wait(dve, s_modb, 16 * (m.b + 1))
                    v.scalar_tensor_tensor(out=x1[:, m.p, :], in0=bank[2][:, D:2 * D], scalar=1.0 / WS,
                                           in1=mod_row("ga"), op0=ALU.mult, op1=ALU.mult)\
                        .then_inc(a_["t1"], 1)
                m = a.back(2)
                if m.inside(NC):
                    wait(dve, a_["sc1"], m.n + 1)
                    wait(dve, a_["pv1"], m.n)
                    mask(1, "m1")
                m = a.back(1)
                if m.inside(NC):
                    wait(dve, a_["exp"], m.n + 1)
                    wait(dve, a_["pv1"], m.n - 1)
                    v.scalar_tensor_tensor(out=feat[:, m.p, :], in0=expo[:, :], scalar=1.0, in1=rb[:, :],
                                           op0=ALU.min, op1=ALU.add).then_inc(a_["f"], 1)
                m = a.back(3)
                if m.inside(NC):
                    wait(dve, a_["x1"], m.n + 1)
                    moments(x1[:, m.p, :], 1, a_["st2"], a_["mv2"], m.n + 1)
                m = a.back(1)
                if m.inside(NC):
                    wait(dve, a_["shi"], m.n + 1)
                    f = feat[:, m.p, :].rearrange("p (q h u d) -> p q h u d", q=2, h=NH, u=1)
                    v.tensor_tensor(qst[:, :, 1:4:2, :], f[:, 0].broadcast_to([P, NH, 2, HD]),
                                    qst[:, :, 0:3:2, :], ALU.subtract)
                    v.tensor_tensor(kst[:, :, 2:4, :], f[:, 1].broadcast_to([P, NH, 2, HD]),
                                    kst[:, :, 0:2, :], ALU.subtract).then_inc(a_["slo"], 1)
                m = a
                if m.inside(NC):
                    wait(dve, s_x[m.c], 16 * (m.b + 1))
                    moments(x_slot(m), 0, a_["st"], a_["mv"], m.n + 1)
                m = a.back(3)
                if m.inside(NC):
                    wait(dve, s_row[m.p], 32 * m.pairs)
                    wait(dve, a_["h2T"], m.n - 1)
                    normalise(x1[:, m.p, :], 1, h2[:, m.p, :], a_["rs2"], a_["xn2"], m.n + 1)
                m = a.back(2)
                if m.inside(NC):
                    if m.c < CPB - 1:
                        wait(dve, a_["state"], (CPB - 1) * m.b + m.c + 1)
                        dst = state[:, 0, :] if m.c == 0 else state_add[:, :]
                        if m.c > 0:
                            wait(dve, a_["stm"], 2 * m.b + m.c - 1)
                        g = lambda t: t.rearrange("p (g n) -> p g n", g=2)
                        hm = headmask[:, :, :].rearrange("p (u h) w -> p u (h w)", u=1)
                        v.tensor_tensor(g(dst), g(bank[4][:, 0:2 * HG * VW]),
                                        hm.broadcast_to([P, 2, HG * VW]), ALU.mult)\
                            .then_inc(a_["stm0" if m.c == 0 else "stt"], 1)
                    wait(dve, a_["pv1"], m.n + 1)
                    o = bank[7][:, 0:NH * VW].rearrange("p (h w) -> p h w", w=VW)
                    v.tensor_scalar(den[:, 0, :], o[:, :, HD], DEN_MIN, None, ALU.max).then_inc(a_["den"], 1)
                    wait(dve, a_["den"], m.n + 1)
                    v.reciprocal(den[:, 1, :], den[:, 0, :]).then_inc(a_["rec"], 1)
                    wait(dve, a_["rec"], m.n + 1)
                    wait(dve, a_["aT"], m.n)
                    v.tensor_tensor(attn[:, :].rearrange("p (h d) -> p h d", d=HD), o[:, :, 0:HD],
                                    den[:, 1, :].rearrange("p (h u) -> p h u", u=1).broadcast_to([P, NH, HD]),
                                    ALU.mult).then_inc(a_["at"], 1)
                m = a
                if m.inside(NC):
                    wait(dve, a_["hT"], m.n - 1)
                    normalise(x_slot(m), 0, xn[:, m.p, :], a_["rs"], a_["xn"], m.n + 1)

            def mask(g, name):
                for odd in range(2):
                    last = v.tensor_tensor(am[:, g, odd, :].rearrange("p (h t) -> p h t", t=P),
                                           bank[5 + odd][:, :].rearrange("p (h t) -> p h t", t=P),
                                           causal[:, :].rearrange("p (u t) -> p u t", u=1).broadcast_to([P, 4, P]),
                                           ALU.mult)
                last.then_inc(a_[name], 1)

            steps_a(dve, step)

            ec = [E, NC]
            def tile(k):
                return stage[:, :, :].rearrange("p q n -> p (q n)")[:, 256 * k:256 * (k + 1)]

            def full(k):
                return tile(k).rearrange("p (e i) -> p e i", e=E)

            def over_e(t):
                return t.rearrange("p e i -> p i e")

            def row(k):
                return small[:, k, :]

            def each_e(r):
                return r.rearrange("p (u i) -> p u i", u=1).broadcast_to([P] + ec)

            def each_i(r):
                return r.rearrange("p (e u) -> p e u", u=1).broadcast_to([P] + ec)

            top, rs, best, r1, r2, cw1, cw2 = (row(k) for k in range(7))
            m1, m2 = row(7), row(8)
            start, cnt, nblk, nblk_c, base = (small[:, k, 0:E] for k in range(9, 14))
            prob, shifted, oh1, oh2, eq, sel, tot, slots = (full(k) for k in range(8))
            lg = logits[:, :, :]

            dve.wait_ge(a_["lge"], NC)
            dve.wait_ge(a_["wlo"], NC)
            link(v.tensor_reduce(top, over_e(lg), AX_X, ALU.max))
            link(v.tensor_tensor(shifted, lg, each_e(top), ALU.subtract))
            marks["shift"] = link.n
            dve.wait_ge(s_act, ACT_EXP2)
            link(v.tensor_reduce(rs, over_e(prob), AX_X, ALU.add))
            link(v.reciprocal(rs, rs))
            link(v.tensor_tensor(prob, prob, each_e(rs), ALU.mult))
            for oh, m_ in ((oh1, m1), (oh2, m2)):
                if oh is oh2:
                    link(v.scalar_tensor_tensor(out=tile(0), in0=tile(2), scalar=-2.0, in1=tile(0),
                                                op0=ALU.mult, op1=ALU.add))
                link(v.tensor_reduce(m_, over_e(prob), AX_X, ALU.max))
                link(v.tensor_tensor(eq, prob, each_e(m_), ALU.is_equal))
                link(v.tensor_tensor(eq, eq, each_i(rev[:, :]), ALU.mult))
                link(v.tensor_reduce(best, over_e(eq), AX_X, ALU.max))
                link(v.tensor_tensor(oh, eq, each_e(best), ALU.is_equal))
            link(v.tensor_tensor(sel, oh1, oh2, ALU.add))
            marks["sel"] = link.n
            link(v.scalar_tensor_tensor(out=rs, in0=m1, scalar=TOP_EPS, in1=m2, op0=ALU.add, op1=ALU.add))
            link(v.reciprocal(rs, rs))
            for cw, m_ in ((cw1, m1), (cw2, m2)):
                link(v.scalar_tensor_tensor(out=cw, in0=m_, scalar=1.0 / WS, in1=rs,
                                            op0=ALU.mult, op1=ALU.mult))
            link(v.memset(w_ones, 1.0))
            dve.wait_ge(s_pe, PE_RANK)
            cum = tile(4)
            link(v.tensor_copy(tile(6), bank[2][:, 0:E * NC]))
            link(v.tensor_tensor_scan(cum, w_ones, tile(6), 0.0, ALU.mult, ALU.add))
            link(v.tensor_tensor(tile(7), bank[1][:, 0:E * NC], cum, ALU.add))
            link(v.tensor_tensor(tile(7), tile(7), tile(6), ALU.subtract))
            cum_e = full(4)[:, :, NC - 1]
            link(v.memset(start, 0.0))
            link(v.tensor_copy(start[:, 1:E], cum_e[:, 0:E - 1]))
            link(v.tensor_tensor(cnt, cum_e, start, ALU.subtract))
            link(v.tensor_tensor(full(6), each_i(cnt), each_e(tile_f[:, :]), ALU.is_gt))
            link(v.tensor_reduce(nblk, full(6), AX_X, ALU.add))
            link(v.tensor_tensor_scan(nblk_c, w_ones[:, 0:E], nblk, 0.0, ALU.mult, ALU.add))
            link(v.tensor_tensor(base, nblk_c, nblk, ALU.subtract))
            link(v.scalar_tensor_tensor(out=base, in0=base, scalar=float(P), in1=start,
                                        op0=ALU.mult, op1=ALU.subtract))
            link(v.tensor_tensor(slots, slots, each_i(base), ALU.add))
            for k, oh in enumerate((oh1, oh2)):
                link(v.tensor_tensor(oh, oh, slots, ALU.mult))
                link(v.tensor_reduce(slot_f[:, 1, k, :], over_e(oh), AX_X, ALU.add))
            link(v.tensor_copy(slot_i[:, 1, :, :], slot_f[:, 1, :, :]))
            link(v.tensor_scalar(slot_i[:, 0, :, :], slot_i[:, 1, :, :], 7, None, ALU.logical_shift_right))
            link(v.tensor_scalar(slot_i[:, 1, :, :], slot_i[:, 1, :, :], P - 1, None, ALU.bitwise_and))
            link(v.tensor_copy(slot_f[:, :, :, :], slot_i[:, :, :, :]))
            marks["slot"] = link.n
            fits = feat[:, :, :].rearrange("p q n -> p (q n)")[:, 0:TB * E].rearrange("p (j e) -> p j e", e=E)
            link(v.tensor_tensor(fits, nblk_c.rearrange("p (u e) -> p u e", u=1).broadcast_to([P, TB, E]),
                                 iota_f[:, 0:TB].rearrange("p (j u) -> p j u", u=1).broadcast_to([P, TB, E]),
                                 ALU.is_le))
            link(v.tensor_reduce(cwT[:, :], fits, AX_X, ALU.add))
            link(v.tensor_scalar(block_e[:, :], cwT[:, :], float(E - 1), None, ALU.min))
            marks["block_e"] = link.n

            def pair(i, n):
                for k in range(2):
                    wait(dve, b_["mm"], n * 2 + k - 1)
                    for q, val in enumerate((id1[:, bass.ds(i, 1)], small[:, 5 + k, bass.ds(i, 1)])):
                        v.tensor_scalar(b_rhs[:, k, q, :], iota_f[:, 0:TB], slot_f[:, 0, k, bass.ds(i, 1)],
                                               val, ALU.is_equal, ALU.mult)
                    v.tensor_scalar(b_one[:, k, :], iota_f[:, :], slot_f[:, 1, k, bass.ds(i, 1)], None,
                                    ALU.is_equal).then_inc(b_["a"], 1)

            pair(0, 0)
            with dve.Fori(1, NC) as i:
                pair(i, i)
            dve.wait_ge(s_pe, PE_TABLE)
            table = bank[7][:, 0:2 * TB].rearrange("p (q j) -> p q j", q=2)
            pad, tok = b_rhs[:, 0, 0, :], b_rhs[:, 0, 1, :]
            link(v.tensor_copy(cwT[:, :], table[:, 1, :]))
            link(v.tensor_scalar(tok, table[:, 0, :], -1.0, None, ALU.add))
            link(v.tensor_scalar(pad, table[:, 0, :], 0.0, float(NOWHERE + 1), ALU.is_equal, ALU.mult))
            link(v.tensor_scalar(gidx[:, :], tok, 0.0, None, ALU.max))
            link(v.tensor_tensor(sidx[:, :], tok, pad, ALU.add))

            def load_gi(m):
                wait(dve, s_g[m.c], 16 * m.b)
                v.tensor_copy(gi[:, m.c:m.c + 1], gidx[:, bass.ds(m.n, 1)]).then_inc(c_["gi"], 1)

            for c in range(3):
                load_gi(At(0, c, UC))

            def step_c(a):
                m = a.back(2)
                if m.inside(MAXB):
                    wait(dve, s_sc, 16 * (m.n - 1))
                    v.tensor_copy(si[:, m.c:m.c + 1], sidx[:, bass.ds(m.n, 1)])
                    wait(dve, c_["y"], m.n + 1)
                    v.scalar_tensor_tensor(out=yw[:, m.p, :], in0=bank[1 + m.p][:, 0:D],
                                           scalar=cwT[:, bass.ds(m.n, 1)], in1=xg[:, m.c, D:2 * D],
                                           op0=ALU.mult, op1=ALU.mult).then_inc(c_["yw"], 1)
                m = a.back(-3)
                if m.inside(MAXB):
                    load_gi(m)
                m = a.back(-1)
                if m.inside(MAXB):
                    xlo(m)
                if a.inside(MAXB):
                    for g, ready, done in ((0, "gA", "glA"), (1, "gB", "glB")):
                        wait(dve, c_[ready], a.n + 1)
                        wait(dve, c_["y"], a.n - 1)
                        h_ = slice(g * 512, g * 512 + 512)
                        v.tensor_tensor(glo[:, a.p, h_], g32[:, a.p, h_], ghi[:, a.p, h_], ALU.subtract)\
                            .then_inc(c_[done], 1)

            def xlo(m):
                wait(dve, c_["xhi"], m.n + 1)
                wait(dve, c_["hB"], m.n - 1)
                v.tensor_tensor(xglo[:, m.p, :], bank[7 * m.p][:, 0:D], xghi[:, m.p, :],
                                ALU.subtract).then_inc(c_["xlo"], 1)

            xlo(At(0, 0, UC))
            steps_c(dve, step_c)

        @block.gpsimd
        def _(pool):
            link = Chain(pool, s_pool)
            g = nc.gpsimd
            link(g.memset(ones[:, :], 1.0))
            link(g.memset(ident16[:, :], 0.0))
            link(g.memset(ident[:, :], 0.0))
            link(g.memset(eps[:, :], LN_EPS))
            link(g.memset(minus_half[:, :], -0.5))
            link(g.memset(headmask[:, :, :], 1.0))
            link(g.memset(vx[:, :, :, HD:VW], 1.0))
            for t in (ident, ident16):
                link(g.affine_select(out=t[:, :], in_=t[:, :], compare_op=ALU.not_equal, fill=1.0, base=0,
                                     pattern=[[-1, P]], channel_multiplier=1))
            for t, base in ((causal, 0), (before, -1)):
                link(g.affine_select(out=t[:, :], in_=ones[:, :], compare_op=ALU.is_ge, fill=0.0, base=base,
                                     pattern=[[1, P]], channel_multiplier=-1))
            for base, sign in ((0, 1), (HD - 1, -1)):
                link(g.affine_select(out=headmask[:, :, :], in_=headmask[:, :, :], compare_op=ALU.is_ge,
                                     fill=0.0, base=base, pattern=[[-HD * sign, HG], [0, VW]],
                                     channel_multiplier=sign))
            link(g.iota(iota_i[:, :], pattern=[[1, P]], base=0, channel_multiplier=0))
            link(g.tensor_copy(iota_f[:, :], iota_i[:, :]))
            assert link.n == POOL_CONST, link.n
            link(g.iota(tile_i[:, :], pattern=[[P, NC]], base=0, channel_multiplier=0))
            link(g.tensor_copy(tile_f[:, :], tile_i[:, :]))
            link(g.iota(tile_i[:, :], pattern=[[P, NC]], base=1, channel_multiplier=1))
            link(g.tensor_copy(id1[:, :], tile_i[:, :]))
            link(g.iota(iota_i[:, 0:E], pattern=[[-1, E]], base=E, channel_multiplier=0))
            link(g.tensor_copy(rev[:, :], iota_i[:, 0:E]))

            def root(k, ready, mid, done, count):
                wait(pool, ready, count)
                g.tensor_tensor(var[:, k:k + 1], mv[:, k, 1:2], eps[:, :], ALU.add).then_inc(mid, 1)
                wait(pool, mid, count)
                g.tensor_tensor(rstd[:, k:k + 1], var[:, k:k + 1], minus_half[:, :], ALU.pow)\
                    .then_inc(done, 1)

            def modulate(t, a, scale, shift, mid, done):
                g.tensor_tensor(t, t, mod_row(scale), ALU.mult).then_inc(a_[mid], 1)
                wait(pool, a_[mid], a.n + 1)
                g.tensor_tensor(t, t, mod_row(shift), ALU.add).then_inc(a_[done], 1)

            def step(a):
                m = a.back(1)
                if m.inside(NC):
                    wait(pool, a_["rope"], m.n + 1)
                    g.tensor_tensor(ra[:, :], ra[:, :], rb[:, :], ALU.add).then_inc(a_["R"], 1)
                m = a.back(3)
                if m.inside(NC):
                    wait(pool, a_["t1"], m.n + 1)
                    g.tensor_tensor(x1[:, m.p, :], x1[:, m.p, :], x_slot(m), ALU.add).then_inc(a_["x1"], 1)
                    root(1, a_["mv2"], a_["ve2"], a_["rs2"], m.n + 1)
                if a.inside(NC):
                    root(0, a_["mv"], a_["ve"], a_["rs"], a.n + 1)
                if m.inside(NC):
                    wait(pool, a_["xn2"], m.n + 1)
                    modulate(h2[:, m.p, :], m, "cb", "sb", "hm2", "h2")
                m = a
                if m.inside(NC):
                    if m.c == 0:
                        wait(pool, s_moda, 16 * (m.b + 1))
                    wait(pool, a_["xn"], m.n + 1)
                    modulate(xn[:, m.p, :], m, "ca", "sa", "hm", "h")
                m = a.back(2)
                if m.inside(NC) and 0 < m.c < CPB - 1:
                    wait(pool, a_["stt"], 2 * m.b + m.c)
                    g.tensor_tensor(state[:, m.p, :], state[:, 1 - m.p, :], state_add[:, :], ALU.add)\
                        .then_inc(a_["stm"], 1)
                m = a.back(1)
                if m.inside(NC):
                    wait(pool, a_["whi"], m.n + 1)
                    carry(pool)
                    g.tensor_scalar(stage[:, m.p, :], stage[:, m.p, :], WS, None, ALU.mult)\
                        .then_inc(a_["wsc"], 1)
                    wait(pool, a_["wsc"], m.n + 1)
                    g.tensor_tensor(piece(m, 1), stage[:, m.p, :], piece(m, 0), ALU.subtract)\
                        .then_inc(a_["wlo"], 1)

            steps_a(pool, step)

            pool.wait_ge(s_row[0], 32 * (NC // 2))
            pool.wait_ge(s_row[1], 32 * (NC // 2))
            pool.wait_ge(s_out[0], 16 * (NC // 2))
            pool.wait_ge(s_out[1], 16 * (NC // 2))

            def gather(m):
                wait(pool, c_["gi"], m.n + 1)
                wait(pool, c_["yw"], m.n - 3)
                carry(pool)
                g.indirect_dma_start(xg[:, m.c, :], None, rows_d,
                                     bass.IndirectOffsetOnAxis(ap=gi[:, m.c:m.c + 1], axis=0))\
                    .then_inc(s_g[m.c], 16)

            gather(At(0, 0, UC))
            gather(At(0, 1, UC))

            def step_c(a):
                m = a.back(2)
                if m.inside(MAXB):
                    wait(pool, c_["yw"], m.n + 1)
                    wait(pool, s_sc, 16 * m.n)
                    carry(pool)
                    g.indirect_dma_start(out_rows, bass.IndirectOffsetOnAxis(ap=si[:, m.c:m.c + 1], axis=0),
                                         yw[:, m.p, :], None, bounds_check=T - 1, oob_is_err=False,
                                         compute_op=ALU.add).then_inc(s_sc, 16)
                m = a.back(-2)
                if m.inside(MAXB):
                    gather(m)

            steps_c(pool, step_c)
            pool.wait_ge(s_sc, 16 * MAXB)

        @block.scalar
        def _(act):
            v = nc.scalar

            def copy(out_, in_, scale=1.0):
                return v.activation(out_, in_, ACT.Copy, scale=scale)

            act.wait_ge(s_ld["c"], 16)
            v.activation(c_exp, c_raw, ACT.Exp, scale=-1.0).then_inc(s_act, 1)
            act.wait_ge(s_ld["wq"], 16)
            copy(wqhi[:, :, :], wq_raw, WS).then_inc(s_act, 1)
            act.wait_ge(s_ld["wo"], 16)
            copy(wohi[:, :, :], wo_raw, WS).then_inc(s_act, 1)
            act.wait_ge(s_pool, POOL_CONST)

            def step(a):
                m = a.back(1)
                if m.inside(NC):
                    wait(act, a_["hT"], m.n + 1)
                    wait(act, a_["qkv"], m.n)
                    copy(hThi[:, :], bank[0][:, 0:D]).then_inc(a_["hhi"], 1)
                m = a.back(2)
                if m.inside(NC):
                    wait(act, a_["T"], m.n + 1)
                    wait(act, a_["sc1"], m.n)
                    copy(kstT[:, :], bank[4][:, :].bitcast(F16)).then_inc(a_["kTs"], 1)
                m = a.back(3)
                if m.inside(NC):
                    wait(act, a_["aT"], m.n + 1)
                    wait(act, a_["pj"], m.n)
                    copy(aThi[:, :], bank[7][:, 0:D]).then_inc(a_["ahi"], 1)
                m = a.back(2)
                if m.inside(NC):
                    wait(act, a_["pv1"], m.n)
                    copy(qT[:, :], bank[2][:, 0:D]).then_inc(a_["qTf"], 1)
                m = a.back(1)
                if m.inside(NC):
                    wait(act, a_["qkv"], m.n + 1)
                    wait(act, a_["pv1"], m.n - 1)
                    copy(vx[:, m.p, :, 0:HD], bank[2][:, 0:D].rearrange("p (h d) -> p h d", d=HD),
                         1.0 / WS).then_inc(a_["v"], 1)
                    wait(act, a_["R"], m.n + 1)
                    v.activation(rb[:, :], ra[:, :], ACT.Relu)
                    wait(act, a_["f"], m.n)
                    v.activation(expo[:, :], ra[:, :], ACT.Exp).then_inc(a_["exp"], 1)
                m = a.back(4)
                if m.inside(NC):
                    wait(act, a_["h2T"], m.n + 1)
                    wait(act, a_["lg"], m.n)
                    copy(h2T[:, :], bank[0][:, 0:D]).then_inc(a_["h2e"], 1)
                m = a.back(1)
                if m.inside(NC):
                    wait(act, a_["f"], m.n + 1)
                    wait(act, a_["T"], m.n)
                    f = feat[:, m.p, :].rearrange("p (q h u d) -> p q h u d", q=2, h=NH, u=1)
                    copy(qst[:, :, 0:3:2, :], f[:, 0].broadcast_to([P, NH, 2, HD]))
                    copy(kst[:, :, 0:2, :], f[:, 1].broadcast_to([P, NH, 2, HD])).then_inc(a_["shi"], 1)
                m = a.back(4)
                if m.inside(NC):
                    wait(act, a_["lg"], m.n + 1)
                    copy(logits[:, :, bass.ds(m.n, 1)],
                         bank[0][:, D:D + E].rearrange("p (e u) -> p e u", u=1)).then_inc(a_["lge"], 1)
                m = a.back(1)
                if m.inside(NC):
                    wait(act, s_w[m.p], 16 * (m.pairs + 1))
                    copy(piece(m, 0), stage[:, m.p, :], WS).then_inc(a_["whi"], 1)

            steps_a(act, step)

            act.wait_ge(s_dve, marks["shift"])
            flat = stage[:, :, :].rearrange("p q n -> p (q n)")
            v.activation(flat[:, 0:256], flat[:, 256:512], ACT.Exp).then_inc(s_act, 1)

            def xhi(m):
                wait(act, c_["xT"], m.n + 1)
                wait(act, c_["hB"], m.n - 1)
                copy(xghi[:, m.p, :], bank[7 * m.p][:, 0:D]).then_inc(c_["xhi"], 1)

            xhi(At(0, 0, UC))

            def step_c(a):
                if a.back(-1).inside(MAXB):
                    xhi(a.back(-1))
                if a.inside(MAXB):
                    for g, ready, done, freed in ((0, "hA", "gA", "glA"), (1, "hB", "gB", "glB")):
                        src = bank[3 + 2 * a.p + g][:, :]
                        h_ = slice(g * 512, g * 512 + 512)
                        wait(act, c_[ready], a.n + 1)
                        wait(act, c_[freed], a.n - 1)
                        v.activation(g32[:, a.p, h_], src, ACT.Gelu, scale=1.0 / WS)
                        wait(act, c_["y"], a.n - 1)
                        v.activation(ghi[:, a.p, h_], src, ACT.Gelu, scale=1.0 / WS).then_inc(c_[done], 1)

            steps_c(act, step_c)

        @block.tensor
        def _(pe):
            t = nc.tensor

            def mm3(dst, xhi_, xlo_, whi, wlo, start=True, stop=True):
                t.matmul(dst, xhi_, whi, start=start, stop=False)
                t.matmul(dst, xhi_, wlo, start=False, stop=False)
                return t.matmul(dst, xlo_, whi, start=False, stop=stop)

            pe.wait_ge(s_pool, POOL_CONST)
            pe.wait_ge(s_dve, marks["silu"])
            pe.wait_ge(s_ld["rw"], 16)
            for i, src in enumerate((c_silu, rw_raw)):
                for k in range(KT):
                    o = (i * KT + k) * B
                    last = t.transpose(bank[0][:, o:o + B], src[:, k * P:(k + 1) * P], ident[0:B, 0:B])
            last.then_inc(s_pe, 1)
            pe.wait_ge(s_dve, marks["t"])
            pe.wait_ge(s_ld["wmod"], 16)
            for j in range(3):
                for k in range(KT):
                    last = t.matmul(bank[1 + j][0:B, :], cT[:, k, :], wmod_raw[:, k, 512 * j:512 * j + 512],
                                    start=(k == 0), stop=(k == KT - 1))
            last.then_inc(s_pe, 1)
            pe.wait_ge(s_dve, marks["wo"])

            def scores(g, name):
                for h in range(HG * g, HG * g + HG):
                    j, odd = h // 2, h % 2
                    rows = slice(64 * odd, 64 * odd + 64)
                    cols = slice(j * P, j * P + P)
                    o = (j % 4) * P
                    last = t.matmul(bank[5 + odd][:, o:o + P], kstT[rows, cols], qstT[rows, cols],
                                    start=True, stop=True)
                last.then_inc(a_[name], 1)

            def attend(m, g, name):
                o = bank[7][:, g * HG * VW:(g + 1) * HG * VW]
                if m.c > 0:
                    t.matmul(o, qT[:, g * P:(g + 1) * P],
                             state[:, 1 - m.p, g * HG * VW:(g + 1) * HG * VW],
                             start=True, stop=False, skip_group_check=True)
                for h in range(HG * g, HG * g + HG):
                    q = (h // 2 % 4) * P
                    last = t.matmul(bank[7][:, h * VW:h * VW + VW], am[:, g, h % 2, q:q + P], vx[:, m.p, h, :],
                                    start=(m.c == 0), stop=True, skip_group_check=True)
                last.then_inc(a_[name], 1)

            def transpose2(dst, src):
                for k in range(KT):
                    last = t.transpose(dst[:, k * P:(k + 1) * P], src[:, k * P:(k + 1) * P], ident[:, :])
                return last

            def step(a):
                m = a.back(1)
                if m.inside(NC):
                    wait(pe, a_["h"], m.n + 1)
                    wait(pe, a_["lge"], m.n - 3)
                    transpose2(bank[0][:, 0:D], xn[:, m.p, :]).then_inc(a_["hT"], 1)
                m = a.back(2)
                if m.inside(NC):
                    wait(pe, a_["slo"], m.n + 1)
                    wait(pe, a_["qTs"], m.n)
                    for src, dst, last_sem in ((qst, bank[3], "Tq"), (kst, bank[4], None)):
                        if src is kst:
                            wait(pe, a_["kTs"], m.n)
                            prev = m.back(1)
                            if prev.inside(NC) and prev.c == 0:
                                wait(pe, a_["stm0"], prev.b + 1)
                            elif prev.inside(NC) and prev.c < CPB - 1:
                                wait(pe, a_["stt"], 2 * prev.b + prev.c)
                        cols = src[:, :, :, :].rearrange("p h c d -> p (h c d)")
                        for j in range(8):
                            last = t.transpose(dst[:, :].bitcast(F16)[:, j * P:(j + 1) * P],
                                               cols[:, j * P:(j + 1) * P], ident16[:, :])
                        if last_sem:
                            last.then_inc(a_[last_sem], 1)
                    wait(pe, a_["v"], m.n + 1)
                    wait(pe, a_["t1"], m.n - 1)
                    transpose2(bank[2][:, 0:D], feat[:, m.p, 0:D]).then_inc(a_["T"], 1)
                m = a.back(3)
                if m.inside(NC):
                    wait(pe, a_["at"], m.n + 1)
                    transpose2(bank[7][:, 0:D], attn[:, :]).then_inc(a_["aT"], 1)
                m = a.back(1)
                if m.inside(NC):
                    wait(pe, a_["hlo"], m.n + 1)
                    wait(pe, a_["rope"], m.n)
                    wait(pe, a_["qTf"], m.n)
                    wait(pe, a_["t1"], m.n - 3)
                    for dst, n0, n1 in ((bank[1][:, :], 0, 2 * D), (bank[2][:, 0:D], 2 * D, 3 * D)):
                        for k in range(KT):
                            c_k = slice(k * P, (k + 1) * P)
                            last = mm3(dst, hThi[:, c_k], hTlo[:, c_k], wqhi[:, k, n0:n1], wqlo[:, k, n0:n1],
                                       start=(k == 0), stop=(k == KT - 1))
                    last.then_inc(a_["qkv"], 1)
                m = a.back(2)
                if m.inside(NC):
                    wait(pe, a_["qTs"], m.n + 1)
                    wait(pe, a_["kTs"], m.n + 1)
                    wait(pe, a_["m1"], m.n)
                    scores(0, "sc0")
                m = a.back(3)
                if m.inside(NC):
                    wait(pe, a_["alo"], m.n + 1)
                    wait(pe, a_["v"], m.n + 3, NC)
                    wait(pe, a_["qTf"], m.n + 2, NC)
                    for k in range(KT):
                        c_k = slice(k * P, (k + 1) * P)
                        last = mm3(bank[2][:, D:2 * D], aThi[:, c_k], aTlo[:, c_k], wohi[:, k, :], wolo[:, k, :],
                                   start=(k == 0), stop=(k == KT - 1))
                    last.then_inc(a_["pj"], 1)
                m = a.back(4)
                if m.inside(NC):
                    wait(pe, a_["h2"], m.n + 1)
                    wait(pe, a_["hlo"], m.n + 4, NC)
                    wait(pe, a_["lge"], m.n)
                    transpose2(bank[0][:, 0:D], h2[:, m.p, :]).then_inc(a_["h2T"], 1)
                m = a.back(2)
                if m.inside(NC):
                    wait(pe, a_["m0"], m.n + 1)
                    scores(1, "sc1")
                m = a.back(4)
                if m.inside(NC):
                    wait(pe, a_["h2e"], m.n + 1)
                    for k in range(KT):
                        last = t.matmul(bank[0][:, D:D + E], h2T[:, k * P:(k + 1) * P], rwT[:, k, :],
                                        start=(k == 0), stop=(k == KT - 1))
                    last.then_inc(a_["lg"], 1)
                m = a.back(2)
                if m.inside(NC):
                    wait(pe, a_["qTf"], m.n + 1)
                    wait(pe, a_["v"], m.n + 1)
                    wait(pe, a_["at"], m.n)
                    if m.c == 1:
                        wait(pe, a_["stm0"], m.b + 1)
                    elif m.c > 1:
                        wait(pe, a_["stm"], 2 * m.b + m.c - 1)
                    attend(m, 0, "pv0")
                    if m.c < CPB - 1:
                        for g in range(2):
                            last = t.matmul(bank[4][:, g * HG * VW:(g + 1) * HG * VW],
                                            feat[:, m.p, D + g * P:D + (g + 1) * P],
                                            vx[:, m.p, g * HG:(g + 1) * HG, :].rearrange("p h w -> p (h w)"),
                                            start=True, stop=True)
                        last.then_inc(a_["state"], 1)
                    wait(pe, a_["m1"], m.n + 1)
                    attend(m, 1, "pv1")

            steps_a(pe, step)

            flat = stage[:, :, :].rearrange("p q n -> p (q n)")
            sel = flat[:, 5 * 256:6 * 256]
            pe.wait_ge(s_dve, marks["sel"])
            t.matmul(bank[1][:, 0:E * NC], before[:, :], sel, start=True, stop=True)
            t.matmul(bank[2][:, 0:E * NC], ones[:, :], sel, start=True, stop=True).then_inc(s_pe, 1)

            def pair(i, n, first=False, final=False):
                for k in range(2):
                    wait(pe, b_["a"], n * 2 + k + 1)
                    last = t.matmul(bank[7][:, 0:2 * TB], b_one[:, k, :],
                                    b_rhs[:, k, :, :].rearrange("p q j -> p (q j)"),
                                    start=(first and k == 0), stop=(final and k == 1))
                    last.then_inc(b_["mm"], 1)

            pair(0, 0, first=True)
            with pe.Fori(1, NC - 1) as i:
                pair(i, i)
            pair(NC - 1, NC - 1, final=True)
            pe.wait_ge(b_["mm"], 2 * NC)
            pe.sem_inc(s_pe, 1)

            def xT(m):
                wait(pe, s_g[m.c], 16 * (m.b + 1))
                wait(pe, c_["xlo"], m.n - 1)
                transpose2(bank[7 * m.p][:, 0:D], xg[:, m.c, 0:D]).then_inc(c_["xT"], 1)

            pe.wait_ge(s_dve, marks["block_e"])
            pe.wait_ge(a_["whi"], NC)
            pe.wait_ge(a_["wlo"], NC)
            xT(At(0, 0, UC))

            def step_c(a):
                if a.back(-1).inside(MAXB):
                    xT(a.back(-1))
                if a.inside(MAXB):
                    e = pe.value_load(block_e[0:1, bass.ds(a.n, 1)], min_val=0, max_val=E - 1)
                    wait(pe, c_["xlo"], a.n + 1)
                    for mt in range(MT):
                        g, q = mt // 4, mt % 4
                        if q == 0:
                            wait(pe, c_["gA" if g == 0 else "gB"], a.n - 1)
                        dst = bank[3 + 2 * a.p + g][:, q * P:(q + 1) * P]
                        for k in range(KT):
                            w_ = bass.ds(e * EW + (k * H + mt * P), P)
                            c_k = slice(k * P, (k + 1) * P)
                            last = mm3w(dst, w1hi[:, w_], w1lo[:, w_], xghi[:, a.p, c_k], xglo[:, a.p, c_k],
                                        start=(k == 0), stop=(k == KT - 1))
                        if q == 3:
                            last.then_inc(c_["hA" if g == 0 else "hB"], 1)
                m = a.back(1)
                if m.inside(MAXB):
                    e = pe.value_load(block_e[0:1, bass.ds(m.n, 1)], min_val=0, max_val=E - 1)
                    wait(pe, c_["yw"], m.n - 1)
                    for mt in range(MT):
                        if mt % 4 == 0:
                            wait(pe, c_["glA" if mt == 0 else "glB"], m.n + 1)
                        w_ = bass.ds(e * EW + mt * D, D)
                        c_m = slice(mt * P, (mt + 1) * P)
                        last = mm3(bank[1 + m.p][:, 0:D], ghi[:, m.p, c_m], glo[:, m.p, c_m], w2hi[:, w_], w2lo[:, w_],
                                   start=(mt == 0), stop=(mt == MT - 1))
                    last.then_inc(c_["y"], 1)

            def mm3w(dst, whi, wlo, xhi_, xlo_, start, stop):
                t.matmul(dst, whi, xhi_, start=start, stop=False)
                t.matmul(dst, whi, xlo_, start=False, stop=False)
                return t.matmul(dst, wlo, xhi_, start=False, stop=stop)

            steps_c(pe, step_c)

        @block.sync
        def _(sp):
            def load_x(a):
                wait(sp, a_["xn"], a.n - CPB + 1)
                carry(sp)
                sp.dma_start(x_slot(a), x_rows[bass.ds(a.n * P, P), :]).then_inc(s_x[a.c], 16)

            def load_mod_a(b):
                wait(sp, a_["h"], b * CPB)
                carry(sp)
                sp.dma_start(mod_a[:, :], mod_d[bass.ds(b, 1), 0:2 * D].broadcast_to([P, 2 * D]))\
                    .then_inc(s_moda, 16)

            def load_mod_b(b):
                wait(sp, a_["h2"], b * CPB)
                carry(sp)
                wait(sp, s_row[1], 32 * (CPB // 2) * b)
                carry(sp)
                sp.dma_start(mod_b[:, :], mod_d[bass.ds(b, 1), 2 * D:6 * D].broadcast_to([P, 4 * D]))\
                    .then_inc(s_modb, 16)

            def load_piece(a):
                wait(sp, a_["wlo"], a.n - 1)
                if a.c < KT:
                    src = w1_v[:, bass.ds(a.b, 1), a.c, :].rearrange("p e h -> p (e h)")
                    dst = stage[:, a.p, :]
                else:
                    q = MT // 2
                    src = w2_v[:, bass.ds(a.b, 1), (a.c - KT) * q:(a.c - KT + 1) * q, :].rearrange(
                        "p e m d -> p (e m) d")
                    dst = stage[:, a.p, :].rearrange("p (m d) -> p m d", m=q)
                carry(sp)
                sp.dma_start(dst, src).then_inc(s_w[a.p], 16)

            sp.dma_start(c_raw, c_in).then_inc(s_ld["c"], 16)
            sp.dma_start(wmod_raw, wmod.rearrange("(k p) n -> p k n", p=P)).then_inc(s_ld["wmod"], 16)
            sp.dma_start(rw_raw, router_w).then_inc(s_ld["rw"], 16)
            load_x(At(0, 0, CPB))
            load_x(At(0, 1, CPB))
            sp.dma_start(wq_raw, w_qkv.rearrange("(k p) n -> p k n", p=P)).then_inc(s_ld["wq"], 16)
            sp.dma_start(cos_t[:, :, :], rope_cos).then_inc(s_ld["cos"], 16)
            sp.dma_start(sin_t[:, :, :, :], rope_sin).then_inc(s_ld["sin"], 16)
            sp.dma_start(wo_raw, w_out.rearrange("(k p) n -> p k n", p=P)).then_inc(s_ld["wo"], 16)
            sp.wait_ge(s_dve, marks["mod"])
            sp.dma_start(mod_d, mod_s).then_inc(s_ms, 16)
            sp.wait_ge(s_ms, 16)
            load_mod_a(0)
            load_mod_b(0)

            def step(a):
                if a.inside(NC):
                    load_piece(a)
                    if a.c == 0 and not (isinstance(a.b, int) and a.b == 0):
                        load_mod_a(a.b)
                if a.back(-2).inside(NC):
                    load_x(a.back(-2))
                m = a.back(3)
                if m.inside(NC):
                    wait(sp, a_["x1"], m.n + 1)
                    carry(sp)
                    sp.dma_start(out_rows[bass.ds(m.n * P, P), :], x1[:, m.p, :]).then_inc(s_out[m.p], 16)
                    wait(sp, a_["h2"], m.n + 1)
                    carry(sp)
                    sp.dma_start(rows_d[bass.ds(m.n * P, P), 0:D], h2[:, m.p, :]).then_inc(s_row[m.p], 16)
                    carry(sp)
                    sp.dma_start(rows_d[bass.ds(m.n * P, P), D:2 * D],
                                 mod_row("gb")).then_inc(s_row[m.p], 16)
                    if m.c == CPB - 1 and m.back(-1).inside(NC):
                        load_mod_b(m.b + 1)

            steps_a(sp, step)


_INS = ["L0_attn_x", "L0_attn_w_qkv", "L0_attn_w_out", "L0_ffn_router_w", "L0_ffn_w1", "L0_ffn_w2",
        "L0_c", "L0_wmod"]


def rope_tables():
    hd2 = HD // 2
    inv = (np.float32(1.0) / np.float32(10000.0) ** (np.arange(hd2, dtype=np.float32) / np.float32(hd2)))
    ang = np.arange(S, dtype=np.float32)[:, None] * inv.astype(np.float32)[None, :]
    scale = np.float32(Q_SCALE / WS)
    cos, sin = np.cos(ang) * scale, np.sin(ang) * scale
    by_place = lambda t: np.ascontiguousarray(
        t.reshape((CPB, P) + t.shape[1:]).swapaxes(0, 1), dtype=np.float32)
    return by_place(cos), by_place(np.stack([-sin, sin], axis=1))


def kernel(**inputs):
    import concourse.bacc as _bacc
    from concourse.bass_utils import run_bass_kernel_spmd as _run

    nc = _bacc.Bacc("TRN2", target_bir_lowering=False, num_devices=1)
    arrays = {f"in_{name}_dram": np.ascontiguousarray(inputs[name]) for name in _INS}
    arrays["rope_cos"], arrays["rope_sin"] = rope_tables()
    args = [nc.dram_tensor(name, a.shape, mybir.dt.from_np(a.dtype), kind="ExternalInput").ap()
            for name, a in arrays.items()]
    args.append(nc.dram_tensor("out_dram", (B, S, D), F32, kind="ExternalOutput").ap())
    adaln_block(nc, *args)
    r = _run(nc, [arrays], core_ids=[0])
    return r.results[0]["out_dram"]
```

```python
from contextlib import ExitStack

import numpy as np

import concourse.bass as bass
from concourse import mybir

ALU = mybir.AluOpType
ACT = mybir.ActivationFunctionType
AX_X = mybir.AxisListType.X
F32 = mybir.dt.float32
F16 = mybir.dt.float16
I32 = mybir.dt.int32
U32 = mybir.dt.uint32

P = 128
B, S, D = 8, 512, 256
NH, HD = 16, 16
E, H = 8, 1024
KT = D // P
MT = H // P
CPB = S // P
NC = B * CPB
T = B * S
VW = HD + 1
HG = 8
EW = KT * H
PIECE = 2 * EW // CPB
MAXB = (2 * T + E * (P - 1)) // P
TB = MAXB + MAXB % 2
LN_EPS = 1e-5
DEN_MIN = 1e-6
TOP_EPS = 1e-9
GATE_MIN = 0.25
WS = 64.0
Q_SCALE = float(HD ** -0.25)
LAG_A = 5
LAG_C = 2
NOWHERE = 2 * T
UC = 4


class At:

    def __init__(self, b, c, unroll):
        self.unroll, self.b, self.c = unroll, b + c // unroll, c % unroll
        self.n = self.b * unroll + self.c
        self.p = self.c % 2
        self.pairs = self.b * (unroll // 2) + self.c // 2

    def back(self, k):
        return At(self.b, self.c - k, self.unroll)

    def inside(self, count):
        return not isinstance(self.n, int) or 0 <= self.n < count


def wait(eng, sem, value, most=None):
    if isinstance(value, int):
        if most is not None:
            value = min(value, most)
        if value <= 0:
            return
    eng.wait_ge(sem, value)


def adaln_block(nc, x, w_qkv, w_out, router_w, w1, w2, c_in, wmod, rope_cos, rope_sin, out):
    ctx = ExitStack()
    with ctx:
        def sb(name, shape, dt=F32):
            return ctx.enter_context(nc.sbuf_tensor(name, shape, dt))

        def sem(name):
            return ctx.enter_context(nc.semaphore(name))

        bank = [ctx.enter_context(nc.psum_tensor(f"bank{i}", [P, 512], F32)) for i in range(8)]
        mod_d = nc.dram_tensor("mod_rows", (B, 6 * D), F32, kind="Internal").ap()
        rows_d = nc.dram_tensor("ffn_rows", (T, 2 * D), F32, kind="Internal").ap()

        w1hi = sb("w1hi", [P, E * EW], F16)
        w1lo = sb("w1lo", [P, E * EW], F16)
        w2hi = sb("w2hi", [P, E * EW], F16)
        w2lo = sb("w2lo", [P, E * EW], F16)
        stage = sb("stage", [P, 2, PIECE])

        ident16 = sb("ident16", [P, P], F16)
        causal = sb("causal", [P, P])
        before = sb("before", [P, P], F16)
        ones = sb("ones", [P, P], F16)
        consts = sb("consts", [P, 2])
        eps, minus_half = consts[:, 0:1], consts[:, 1:2]
        cos_t = sb("cos_t", [P, CPB, HD // 2])
        sin_t = sb("sin_t", [P, CPB, 2, HD // 2])
        wqhi = sb("wqhi", [P, KT, 3 * D], F16)
        wqlo = sb("wqlo", [P, KT, 3 * D], F16)
        wohi = sb("wohi", [P, KT, D], F16)
        wolo = sb("wolo", [P, KT, D], F16)
        rwhi = sb("rwhi", [P, KT, E], F16)
        rwlo = sb("rwlo", [P, KT, E], F16)
        mod_a = sb("mod_a", [P, 2 * D])
        mod_g = sb("mod_g", [P, D])
        mod_b = sb("mod_b", [P, 2 * D])
        logits = sb("logits", [P, E, NC])

        xt = sb("xt", [P, 2 * CPB * D])
        st = sb("st", [P, 2, 6])
        mv = sb("mv", [P, 2, 2])
        var = sb("var", [P, 2])
        rstd = sb("rstd", [P, 2])
        h16 = sb("h16", [P, 2, D], F16)
        hT = sb("hT", [P, 2, D], F16)
        ra = sb("ra", [P, 2 * D])
        rb = sb("rb", [P, 2 * D])
        h = rb[:, 0:D]
        feat = sb("feat", [P, 2 * D])
        v16 = sb("v16", [P, CPB, 2, NH, VW], F16)
        qst = sb("qst", [P, NH, 4, HD], F16)
        kst = sb("kst", [P, NH, 4, HD], F16)
        qstT = sb("qstT", [P, 8 * P], F16)
        kstT = sb("kstT", [P, 8 * P], F16)
        am = sb("am", [P, 2, 2, 4 * P])
        amhi = sb("amhi", [P, 2, 2, 4 * P], F16)
        amlo = sb("amlo", [P, 2, 2, 4 * P], F16)
        state = sb("state", [P, 2, 2, NH * VW], F16)
        den = sb("den", [P, 2, NH])
        attn = ra[:, 0:D]
        a16 = sb("a16", [P, 2, D], F16)
        aT = sb("aT", [P, 2, D], F16)
        x1 = sb("x1", [P, 2, D])
        h2 = sb("h2", [P, D])
        h2_16 = sb("h2_16", [P, 2, 2, D], F16)
        h2T = sb("h2T", [P, 2, D], F16)

        iota_f = sb("iota_f", [P, P])
        tile_f = sb("tile_f", [P, NC])
        id1 = sb("id1", [P, NC])
        small = feat[:, 0:14 * NC].rearrange("p (k i) -> p k i", k=14)
        slot_i = ra[:, 0:4 * NC].bitcast(I32).rearrange("p (u k i) -> p u k i", u=2, k=2)
        slot_f = ra[:, 4 * NC:8 * NC].rearrange("p (u k i) -> p u k i", u=2, k=2)
        w_q = wqlo[:, :, :].rearrange("p k n -> p (k n)").bitcast(F32)
        block_e, gidx, sidx, cwT = (w_q[:, i * TB:(i + 1) * TB] for i in range(4))
        block_e, gidx, sidx = (t.bitcast(I32) for t in (block_e, gidx, sidx))
        gi = sb("gi", [P, UC], U32)
        si = sb("si", [P, UC], U32)

        xg = xt[:, :].rearrange("p (q n) -> p q n", q=UC)
        g32 = am[:, :, :, :].rearrange("p g o n -> p g (o n)")
        def halves(t):
            return t.rearrange("p (q n) -> p q n", q=2)
        ghi = halves(amhi[:, :, :, :].rearrange("p g o n -> p (g o n)"))
        glo = halves(amlo[:, :, :, :].rearrange("p g o n -> p (g o n)"))
        x16 = qstT[:, :].rearrange("p (q n) -> p q n", q=2)
        yw = x1
        b_rhs = qst[:, :, :, :].rearrange("p h c d -> p (h c d)").bitcast(F32)[:, 0:4 * TB].rearrange(
            "p (k q j) -> p k q j", k=2, q=2)
        b_one = kst[:, :, :, :].rearrange("p h c d -> p (h c d)").bitcast(F32)[:, 0:2 * P].rearrange(
            "p (k t) -> p k t", k=2)
        w_ones = rb[:, 0:E * NC]
        rev = sb("rev", [P, E])

        half = E // 2 * EW
        late = [t[:, half:2 * half].bitcast(F32) for t in (w2hi, w2lo, w1lo)]
        wmod_raw = late[0][:, 0:KT * 6 * D].rearrange("p (k n) -> p k n", k=KT)
        wq_raw = late[1][:, 0:KT * 3 * D].rearrange("p (k n) -> p k n", k=KT)
        wo_raw = late[1][:, 1536:1536 + KT * D].rearrange("p (k n) -> p k n", k=KT)
        rw_raw = late[1][0:E, 2048:2048 + D]
        ident = late[2][:, 2048:2048 + P]
        iota_i = late[2][:, 2048 + P:2048 + 2 * P].bitcast(I32)
        tile_i = late[2][:, 2048 + 2 * P:2048 + 2 * P + NC].bitcast(I32)
        c_raw = late[1][0:B, 2304:2304 + D]
        c_exp = late[1][0:B, 2560:2560 + D]
        c_silu = late[1][0:B, 2816:2816 + D]
        cT = late[1][:, 3072:3072 + KT * B].rearrange("p (k b) -> p k b", k=KT)
        mod_s = late[2][0:B, 0:6 * D]
        gate_s = late[2][0:B, 1536:1536 + D]
        gate_a = late[2][0:B, 1792:1792 + D]

        def counters(prefix, names):
            return {k: sem(prefix + k) for k in names.split()}

        a_ = counters("a_", "st mv ve rs xn hm h hhi hlo hT hTe v vhi vlo qk rope R exp f shi slo Tq qTs Tk kTs"
                            " state sth stl sc0 m0 mh0 ml0 sc1 m1 mh1 ml1 pv0 pv1 den rec at ahi alo aT aTe pj"
                            " t1 x1 st2 mv2 ve2 rs2 xn2 hm2 h2 h2hi h2lo h2T h2Te lg lge whi wlo")
        s_x = [sem(f"s_x{c}") for c in range(CPB)]
        s_moda = sem("s_moda")
        s_modb = sem("s_modb")
        s_modg = sem("s_modg")
        s_gb = sem("s_gb")
        s_w = [sem("s_w0"), sem("s_w1")]
        s_out = [sem("s_out0"), sem("s_out1")]
        s_row = [sem("s_row0"), sem("s_row1")]
        s_ld = {k: sem("s_ld_" + k) for k in ("c", "wmod", "wq", "wo", "rw", "cos", "sin")}
        s_pool = sem("s_pool")
        s_dve = sem("s_dve")
        s_pe = sem("s_pe")
        s_act = sem("s_act")
        s_ms = sem("s_ms")
        b_ = counters("b_", "a mm")
        s_carry = sem("s_carry")
        c_ = counters("c_", "gi xT xTe hA hB gA gB glA glB y yw")
        s_g = [sem(f"s_g{q}") for q in range(UC)]
        s_sc = sem("s_sc")

        x_rows = x.rearrange("b s d -> (b s) d")
        out_rows = out.rearrange("b s d -> (b s) d")
        w1_v = w1.rearrange("e (k p) h -> p e k h", p=P)
        w2_v = w2.rearrange("e (m p) d -> p e m d", p=P)
        MOD = {k: i * D for i, k in enumerate(("sa", "ca", "ga", "sb", "cb", "gb"))}

        def x_slot(a):
            return xt[:, bass.ds((a.b % 2) * (CPB * D) + a.c * D, D)]

        def own(t, u):
            return t.rearrange("p (j u w) -> p j u w", u=2, w=VW)[64 * u:64 * u + 64, :, u, :]

        def steps_a(eng, step):
            for c in range(2 * CPB):
                step(At(0, c, CPB))
            with eng.Fori(2, B - 1) as b:
                for c in range(CPB):
                    step(At(b, c, CPB))
            for c in range(CPB + LAG_A):
                step(At(B - 1, c, CPB))

        def steps_c(eng, step):
            for c in range(UC):
                step(At(0, c, UC))
            with eng.Fori(1, MAXB // UC) as b:
                for c in range(UC):
                    step(At(b, c, UC))
            for c in range(MAXB % UC + LAG_C):
                step(At(MAXB // UC, c, UC))

        class Chain:

            def __init__(self, eng, sem_):
                self.eng, self.sem, self.n = eng, sem_, 0

            def __call__(self, ins):
                self.n += 1
                ins.then_inc(self.sem, 1)
                self.eng.wait_ge(self.sem, self.n)

        def piece(a, part):
            t = (w1hi, w1lo, w2hi, w2lo)[2 * (a.c // KT) + part]
            return t[:, bass.ds(a.b * EW + (a.c % KT) * PIECE, PIECE)]

        block = ctx.enter_context(nc.Block())

        marks = {}

        def carry(eng):
            eng.sem_inc(s_carry, 1)

        POOL_CONST = 16
        ACT_EXP, ACT_W, ACT_EXP2 = 1, 3, 4
        PE_T, PE_MOD, PE_RANK, PE_TABLE = 1, 2, 3, 4

        @block.vector
        def _(dve):
            link = Chain(dve, s_dve)
            v = nc.vector

            dve.wait_ge(s_act, ACT_EXP)
            link(v.tensor_scalar(c_exp, c_exp, 1.0, None, ALU.add))
            link(v.reciprocal(c_exp, c_exp))
            link(v.tensor_tensor(c_silu, c_raw, c_exp, ALU.mult))
            marks["silu"] = link.n
            dve.wait_ge(s_pe, PE_T)
            link(v.tensor_copy(cT, bank[0][:, 0:KT * B].rearrange("p (k b) -> p k b", k=KT)))
            rw_ps = bank[0][:, KT * B:KT * (B + E)].rearrange("p (k e) -> p k e", k=KT)
            link(v.tensor_scalar(rwhi[:, :, :], rw_ps, WS, None, ALU.mult))
            link(v.scalar_tensor_tensor(out=rwlo[:, :, :], in0=rw_ps, scalar=WS, in1=rwhi[:, :, :],
                                        op0=ALU.mult, op1=ALU.subtract))
            marks["t"] = link.n
            dve.wait_ge(s_pe, PE_MOD)
            for k, add in (("sa", 0.0), ("ca", 1.0), ("ga", None), ("sb", 0.0), ("cb", 1.0), ("gb", None)):
                o = MOD[k]
                src, dst = bank[1 + o // 512][0:B, o % 512:o % 512 + D], mod_s[:, o:o + D]
                if add is None:
                    link(v.tensor_scalar(gate_s, src, 0.0, 2.0, ALU.is_ge, ALU.mult))
                    link(v.tensor_copy(gate_a, src))
                    link(v.scalar_tensor_tensor(out=gate_a, in0=gate_a, scalar=-1.0, in1=gate_a,
                                                op0=ALU.mult, op1=ALU.max))
                    link(v.tensor_scalar(gate_a, gate_a, GATE_MIN, None, ALU.max))
                    link(v.scalar_tensor_tensor(out=dst, in0=gate_s, scalar=-1.0, in1=gate_a,
                                                op0=ALU.add, op1=ALU.mult))
                else:
                    link(v.tensor_scalar(dst, src, add, None, ALU.add))
            marks["mod"] = link.n
            dve.wait_ge(s_act, ACT_W)
            for raw, hi, lo in ((wq_raw, wqhi, wqlo), (wo_raw, wohi, wolo)):
                link(v.scalar_tensor_tensor(out=lo[:, :, :], in0=raw, scalar=WS, in1=hi[:, :, :],
                                            op0=ALU.mult, op1=ALU.subtract))
            marks["wo"] = link.n
            dve.wait_ge(s_pool, POOL_CONST)
            def moments(src, k, done_stats, done, count):
                v.bn_stats(st[:, k, :], src).then_inc(done_stats, 1)
                wait(dve, done_stats, count)
                carry(dve)
                v.bn_aggr(mv[:, k, :], st[:, k, :]).then_inc(done, 1)

            def normalise(src, k, dst, rs, done, count):
                wait(dve, rs, count)
                v.tensor_scalar(dst, src, mv[:, k, 0:1], rstd[:, k:k + 1], ALU.subtract, ALU.mult)\
                    .then_inc(done, 1)

            def low(dst, src, high, done):
                v.tensor_tensor(dst, src, high, ALU.subtract).then_inc(a_[done], 1)

            def mask(m, g):
                wait(dve, a_[f"sc{g}"], m.n + 1)
                wait(dve, a_[f"ml{g}"], m.n)
                for odd in range(2):
                    last = v.tensor_tensor(am[:, g, odd, :].rearrange("p (h t) -> p h t", t=P),
                                           bank[5 + odd][:, :].rearrange("p (h t) -> p h t", t=P),
                                           causal[:, :].rearrange("p (u t) -> p u t", u=1).broadcast_to([P, 4, P]),
                                           ALU.mult)
                last.then_inc(a_[f"m{g}"], 1)

            def step(a):
                n0, n1, n2, n3, n4 = a, a.back(1), a.back(2), a.back(3), a.back(4)
                if n0.inside(NC):
                    wait(dve, s_x[n0.c], 16 * (n0.b + 1))
                    moments(x_slot(n0), 0, a_["st"], a_["mv"], n0.n + 1)
                if n1.inside(NC):
                    wait(dve, a_["shi"], n1.n + 1)
                    f = feat[:, :].rearrange("p (q h u d) -> p q h u d", q=2, h=NH, u=1)
                    v.tensor_tensor(qst[:, :, 1:4:2, :], f[:, 0].broadcast_to([P, NH, 2, HD]),
                                    qst[:, :, 0:3:2, :], ALU.subtract)
                    low(kst[:, :, 2:4, :], f[:, 1].broadcast_to([P, NH, 2, HD]), kst[:, :, 0:2, :], "slo")
                if n0.inside(NC):
                    wait(dve, a_["hlo"], n0.n)
                    normalise(x_slot(n0), 0, h[:, :], a_["rs"], a_["xn"], n0.n + 1)
                if n4.inside(NC):
                    wait(dve, a_["h2lo"], n4.n)
                    normalise(x1[:, n4.p, :], 1, h2[:, :], a_["rs2"], a_["xn2"], n4.n + 1)
                if n0.inside(NC):
                    wait(dve, a_["whi"], n0.n + 1)
                    carry(dve)
                    v.scalar_tensor_tensor(out=piece(n0, 1), in0=stage[:, n0.p, :], scalar=WS,
                                           in1=piece(n0, 0), op0=ALU.mult, op1=ALU.subtract)\
                        .then_inc(a_["wlo"], 1)
                    wait(dve, a_["hhi"], n0.n + 1)
                    wait(dve, a_["hT"], n0.n)
                    low(h16[:, 1, :], h[:, :], h16[:, 0, :], "hlo")
                if n1.inside(NC):
                    wait(dve, a_["Tk"], n1.n + 1)
                    wait(dve, a_["sc1"], n1.n)
                    v.tensor_copy(kstT[:, :], bank[3][:, :].bitcast(F16)).then_inc(a_["kTs"], 1)
                if n3.inside(NC):
                    wait(dve, a_["pj"], n3.n + 1)
                    wait(dve, s_out[n3.p], 16 * n3.pairs)
                    wait(dve, s_modg, 16 * (n3.b + 1))
                    v.scalar_tensor_tensor(out=x1[:, n3.p, :], in0=bank[2][:, 0:D], scalar=1.0 / WS,
                                           in1=mod_g[:, :], op0=ALU.mult, op1=ALU.mult)\
                        .then_inc(a_["t1"], 1)
                if n1.inside(NC):
                    mask(n1, 0)
                if n0.inside(NC):
                    wait(dve, a_["vhi"], n0.n + 1)
                    v.scalar_tensor_tensor(out=v16[:, n0.c, 1, :, 0:HD],
                                           in0=bank[2][:, 0:D].rearrange("p (h d) -> p h d", d=HD), scalar=1.0 / WS,
                                           in1=v16[:, n0.c, 0, :, 0:HD], op0=ALU.mult, op1=ALU.subtract)\
                        .then_inc(a_["vlo"], 1)
                if n3.inside(NC):
                    wait(dve, a_["x1"], n3.n + 1)
                    v.bn_stats(st[:, 1, :], x1[:, n3.p, :]).then_inc(a_["st2"], 1)
                if n0.inside(NC):
                    wait(dve, a_["qk"], n0.n + 1)
                    wait(dve, a_["exp"], n0.n)
                    wait(dve, a_["alo"], n0.n - 2)
                    half_d = HD // 2
                    qk = bank[1][:, :].rearrange("p (h o d) -> p h o d", o=2, d=half_d)
                    rbv = rb[:, :].rearrange("p (h o d) -> p h o d", o=2, d=half_d)
                    v.tensor_tensor(ra[:, :].rearrange("p (h d) -> p h d", d=half_d),
                                    bank[1][:, :].rearrange("p (h d) -> p h d", d=half_d),
                                    cos_t[:, n0.c:n0.c + 1, :].broadcast_to([P, 4 * NH, half_d]), ALU.mult)
                    for o in range(2):
                        last = v.tensor_tensor(rbv[:, :, o, :], qk[:, :, 1 - o, :],
                                               sin_t[:, n0.c, o:o + 1, :].broadcast_to([P, 2 * NH, half_d]),
                                               ALU.mult)
                    last.then_inc(a_["rope"], 1)
                if n3.inside(NC):
                    wait(dve, a_["st2"], n3.n + 1)
                    wait(dve, a_["xn2"], n3.n)
                    carry(dve)
                    v.bn_aggr(mv[:, 1, :], st[:, 1, :]).then_inc(a_["mv2"], 1)
                if n4.inside(NC):
                    wait(dve, a_["h2hi"], n4.n + 1)
                    low(h2_16[:, n4.p, 1, :], h2[:, :], h2_16[:, n4.p, 0, :], "h2lo")
                if n1.inside(NC) and n1.c < CPB - 1:
                    wait(dve, a_["sth"], (CPB - 1) * n1.b + n1.c + 1)
                    v.tensor_tensor(own(state[:, n1.p, 1, :], 0), own(bank[4][:, 0:NH * VW], 0),
                                    own(state[:, n1.p, 0, :], 0), ALU.subtract)
                    low(own(state[:, n1.p, 1, :], 1), own(bank[4][:, 0:NH * VW], 1),
                        own(state[:, n1.p, 0, :], 1), "stl")
                if n1.inside(NC):
                    mask(n1, 1)
                o = bank[7][:, 0:NH * VW].rearrange("p (h w) -> p h w", w=VW)
                if n2.inside(NC):
                    wait(dve, a_["pv1"], n2.n + 1)
                    v.tensor_scalar(den[:, 0, :], o[:, :, HD], DEN_MIN, None, ALU.max).then_inc(a_["den"], 1)
                if n0.inside(NC):
                    wait(dve, a_["exp"], n0.n + 1)
                    v.scalar_tensor_tensor(out=feat[:, :], in0=feat[:, :], scalar=1.0, in1=rb[:, :],
                                           op0=ALU.min, op1=ALU.add).then_inc(a_["f"], 1)
                if n2.inside(NC):
                    wait(dve, a_["den"], n2.n + 1)
                    v.reciprocal(den[:, 1, :], den[:, 0, :]).then_inc(a_["rec"], 1)
                    wait(dve, a_["rec"], n2.n + 1)
                    wait(dve, a_["exp"], n2.n + 3, NC)
                    v.tensor_tensor(attn[:, :].rearrange("p (h d) -> p h d", d=HD), o[:, :, 0:HD],
                                    den[:, 1, :].rearrange("p (h u) -> p h u", u=1).broadcast_to([P, NH, HD]),
                                    ALU.mult).then_inc(a_["at"], 1)

            steps_a(dve, step)

            ec = [E, NC]
            def tile(k):
                return stage[:, :, :].rearrange("p q n -> p (q n)")[:, 256 * k:256 * (k + 1)]

            def full(k):
                return tile(k).rearrange("p (e i) -> p e i", e=E)

            def over_e(t):
                return t.rearrange("p e i -> p i e")

            def row(k):
                return small[:, k, :]

            def each_e(r):
                return r.rearrange("p (u i) -> p u i", u=1).broadcast_to([P] + ec)

            def each_i(r):
                return r.rearrange("p (e u) -> p e u", u=1).broadcast_to([P] + ec)

            top, rs, best, r1, r2, cw1, cw2 = (row(k) for k in range(7))
            m1, m2 = row(7), row(8)
            start, cnt, nblk, nblk_c, base = (small[:, k, 0:E] for k in range(9, 14))
            prob, shifted, oh1, oh2, eq, sel, tot, slots = (full(k) for k in range(8))
            lg = logits[:, :, :]

            dve.wait_ge(a_["lge"], NC)
            dve.wait_ge(a_["wlo"], NC)
            link(v.tensor_reduce(top, over_e(lg), AX_X, ALU.max))
            link(v.tensor_tensor(shifted, lg, each_e(top), ALU.subtract))
            marks["shift"] = link.n
            dve.wait_ge(s_act, ACT_EXP2)
            link(v.tensor_reduce(rs, over_e(prob), AX_X, ALU.add))
            link(v.reciprocal(rs, rs))
            link(v.tensor_tensor(prob, prob, each_e(rs), ALU.mult))
            for oh, m_ in ((oh1, m1), (oh2, m2)):
                if oh is oh2:
                    link(v.scalar_tensor_tensor(out=tile(0), in0=tile(2), scalar=-2.0, in1=tile(0),
                                                op0=ALU.mult, op1=ALU.add))
                link(v.tensor_reduce(m_, over_e(prob), AX_X, ALU.max))
                link(v.tensor_tensor(eq, prob, each_e(m_), ALU.is_equal))
                link(v.tensor_tensor(eq, eq, each_i(rev[:, :]), ALU.mult))
                link(v.tensor_reduce(best, over_e(eq), AX_X, ALU.max))
                link(v.tensor_tensor(oh, eq, each_e(best), ALU.is_equal))
            link(v.tensor_tensor(tile(5)[:, 0:E * NC // 2].bitcast(F16).rearrange("p (e i) -> p e i", e=E),
                                 oh1, oh2, ALU.add))
            marks["sel"] = link.n
            link(v.scalar_tensor_tensor(out=rs, in0=m1, scalar=TOP_EPS, in1=m2, op0=ALU.add, op1=ALU.add))
            link(v.reciprocal(rs, rs))
            for cw, m_ in ((cw1, m1), (cw2, m2)):
                link(v.scalar_tensor_tensor(out=cw, in0=m_, scalar=1.0 / WS, in1=rs,
                                            op0=ALU.mult, op1=ALU.mult))
            link(v.memset(w_ones, 1.0))
            dve.wait_ge(s_pe, PE_RANK)
            cum = tile(4)
            link(v.tensor_copy(tile(6), bank[2][:, 0:E * NC]))
            link(v.tensor_tensor_scan(cum, w_ones, tile(6), 0.0, ALU.mult, ALU.add))
            link(v.tensor_tensor(tile(7), bank[1][:, 0:E * NC], cum, ALU.add))
            link(v.tensor_tensor(tile(7), tile(7), tile(6), ALU.subtract))
            cum_e = full(4)[:, :, NC - 1]
            link(v.memset(start, 0.0))
            link(v.tensor_copy(start[:, 1:E], cum_e[:, 0:E - 1]))
            link(v.tensor_tensor(cnt, cum_e, start, ALU.subtract))
            link(v.tensor_tensor(full(6), each_i(cnt), each_e(tile_f[:, :]), ALU.is_gt))
            link(v.tensor_reduce(nblk, full(6), AX_X, ALU.add))
            link(v.tensor_tensor_scan(nblk_c, w_ones[:, 0:E], nblk, 0.0, ALU.mult, ALU.add))
            link(v.tensor_tensor(base, nblk_c, nblk, ALU.subtract))
            link(v.scalar_tensor_tensor(out=base, in0=base, scalar=float(P), in1=start,
                                        op0=ALU.mult, op1=ALU.subtract))
            link(v.tensor_tensor(slots, slots, each_i(base), ALU.add))
            for k, oh in enumerate((oh1, oh2)):
                link(v.tensor_tensor(oh, oh, slots, ALU.mult))
                link(v.tensor_reduce(slot_f[:, 1, k, :], over_e(oh), AX_X, ALU.add))
            link(v.tensor_copy(slot_i[:, 1, :, :], slot_f[:, 1, :, :]))
            link(v.tensor_scalar(slot_i[:, 0, :, :], slot_i[:, 1, :, :], 7, None, ALU.logical_shift_right))
            link(v.tensor_scalar(slot_i[:, 1, :, :], slot_i[:, 1, :, :], P - 1, None, ALU.bitwise_and))
            link(v.tensor_copy(slot_f[:, :, :, :], slot_i[:, :, :, :]))
            marks["slot"] = link.n
            fits = xt[:, 0:TB * E].rearrange("p (j e) -> p j e", e=E)
            link(v.tensor_tensor(fits, nblk_c.rearrange("p (u e) -> p u e", u=1).broadcast_to([P, TB, E]),
                                 iota_f[:, 0:TB].rearrange("p (j u) -> p j u", u=1).broadcast_to([P, TB, E]),
                                 ALU.is_le))
            link(v.tensor_reduce(cwT[:, :], fits, AX_X, ALU.add))
            link(v.tensor_scalar(cwT[:, :], cwT[:, :], float(E - 1), None, ALU.min))
            four = cwT.rearrange("p (g c) -> p g c", c=UC)
            digits = xt[:, 1024:1024 + TB // UC]
            link(v.tensor_copy(digits, four[:, :, UC - 1]))
            for c in range(UC - 2, -1, -1):
                link(v.scalar_tensor_tensor(out=digits, in0=digits, scalar=float(E), in1=four[:, :, c],
                                            op0=ALU.mult, op1=ALU.add))
            link(v.scalar_tensor_tensor(out=digits[:, 1:], in0=four[:, 0:-1, UC - 1], scalar=float(E ** UC),
                                        in1=digits[:, 1:], op0=ALU.mult, op1=ALU.add))
            link(v.tensor_copy(block_e[:, 0:TB // UC], digits))
            marks["block_e"] = link.n

            def pair(i, n):
                for k in range(2):
                    wait(dve, b_["mm"], n * 2 + k - 1)
                    for q, val in enumerate((id1[:, bass.ds(i, 1)], small[:, 5 + k, bass.ds(i, 1)])):
                        v.tensor_scalar(b_rhs[:, k, q, :], iota_f[:, 0:TB], slot_f[:, 0, k, bass.ds(i, 1)],
                                               val, ALU.is_equal, ALU.mult)
                    v.tensor_scalar(b_one[:, k, :], iota_f[:, :], slot_f[:, 1, k, bass.ds(i, 1)], None,
                                    ALU.is_equal).then_inc(b_["a"], 1)

            pair(0, 0)
            with dve.Fori(1, NC) as i:
                pair(i, i)
            dve.wait_ge(s_pe, PE_TABLE)
            table = bank[7][:, 0:2 * TB].rearrange("p (q j) -> p q j", q=2)
            pad, tok = b_rhs[:, 0, 0, :], b_rhs[:, 0, 1, :]
            link(v.tensor_copy(cwT[:, :], table[:, 1, :]))
            link(v.tensor_scalar(tok, table[:, 0, :], -1.0, None, ALU.add))
            link(v.tensor_scalar(pad, table[:, 0, :], 0.0, float(NOWHERE + 1), ALU.is_equal, ALU.mult))
            link(v.tensor_scalar(gidx[:, :], tok, 0.0, None, ALU.max))
            link(v.tensor_tensor(sidx[:, :], tok, pad, ALU.add))

            def load_gi(m):
                wait(dve, s_g[m.c], 16 * m.b)
                v.tensor_copy(gi[:, m.c:m.c + 1], gidx[:, bass.ds(m.n, 1)]).then_inc(c_["gi"], 1)

            for c in range(3):
                load_gi(At(0, c, UC))
            dve.wait_ge(c_["xT"], 1)
            v.tensor_copy(x16[:, 0, :], bank[0][:, 0:D].bitcast(F16)).then_inc(c_["xTe"], 1)

            def step_c(a):
                m = a.back(2)
                if m.inside(MAXB):
                    wait(dve, s_sc, 16 * (m.n - 1))
                    v.tensor_copy(si[:, m.c:m.c + 1], sidx[:, bass.ds(m.n, 1)])
                    wait(dve, c_["y"], m.n + 1)
                    v.scalar_tensor_tensor(out=yw[:, m.p, :], in0=bank[1 + m.p][:, 0:D],
                                           scalar=cwT[:, bass.ds(m.n, 1)], in1=xg[:, m.c, D:2 * D],
                                           op0=ALU.mult, op1=ALU.mult).then_inc(c_["yw"], 1)
                m = a.back(-3)
                if m.inside(MAXB):
                    load_gi(m)
                m = a.back(-1)
                if m.inside(MAXB):
                    wait(dve, c_["xT"], m.n + 1)
                    wait(dve, c_["hB"], m.n - 1)
                    v.tensor_copy(x16[:, m.p, :], bank[7 * m.p][:, 0:D].bitcast(F16)).then_inc(c_["xTe"], 1)
                if a.inside(MAXB):
                    for g, ready, done in ((0, "gA", "glA"), (1, "gB", "glB")):
                        wait(dve, c_[ready], a.n + 1)
                        wait(dve, c_["y"], a.n - 1)
                        h_ = slice(g * 512, g * 512 + 512)
                        v.tensor_tensor(glo[:, a.p, h_], g32[:, a.p, h_], ghi[:, a.p, h_], ALU.subtract)\
                            .then_inc(c_[done], 1)

            steps_c(dve, step_c)

        @block.gpsimd
        def _(pool):
            link = Chain(pool, s_pool)
            g = nc.gpsimd
            for t in (ones, before, causal):
                link(g.memset(t[:, :], 1.0))
            link(g.memset(ident16[:, :], 0.0))
            link(g.memset(ident[:, :], 0.0))
            link(g.memset(eps[:, :], LN_EPS))
            link(g.memset(minus_half[:, :], -0.5))
            link(g.memset(v16[:, :, 0, :, HD:VW], 1.0))
            link(g.memset(v16[:, :, 1, :, HD:VW], 0.0))
            link(g.memset(state[:, :, :, :], 0.0))
            for t in (ident, ident16):
                link(g.affine_select(out=t[:, :], in_=t[:, :], compare_op=ALU.not_equal, fill=1.0, base=0,
                                     pattern=[[-1, P]], channel_multiplier=1))
            for t, base in ((causal, 0), (before, -1)):
                link(g.affine_select(out=t[:, :], in_=t[:, :], compare_op=ALU.is_ge, fill=0.0, base=base,
                                     pattern=[[1, P]], channel_multiplier=-1))
            link(g.iota(iota_i[:, :], pattern=[[1, P]], base=0, channel_multiplier=0))
            link(g.tensor_copy(iota_f[:, :], iota_i[:, :]))
            assert link.n == POOL_CONST, link.n
            link(g.iota(tile_i[:, :], pattern=[[P, NC]], base=0, channel_multiplier=0))
            link(g.tensor_copy(tile_f[:, :], tile_i[:, :]))
            link(g.iota(tile_i[:, :], pattern=[[P, NC]], base=1, channel_multiplier=1))
            link(g.tensor_copy(id1[:, :], tile_i[:, :]))
            link(g.iota(iota_i[:, 0:E], pattern=[[-1, E]], base=E, channel_multiplier=0))
            link(g.tensor_copy(rev[:, :], iota_i[:, 0:E]))

            def root(k, ready, mid, done, count):
                wait(pool, ready, count)
                g.tensor_tensor(var[:, k:k + 1], mv[:, k, 1:2], eps[:, :], ALU.add).then_inc(mid, 1)
                wait(pool, mid, count)
                g.tensor_tensor(rstd[:, k:k + 1], var[:, k:k + 1], minus_half[:, :], ALU.pow)\
                    .then_inc(done, 1)

            def modulate(t, m, rows, mid, done):
                g.tensor_tensor(t, t, rows[:, D:2 * D], ALU.mult).then_inc(a_[mid], 1)
                wait(pool, a_[mid], m.n + 1)
                g.tensor_tensor(t, t, rows[:, 0:D], ALU.add).then_inc(a_[done], 1)

            def scores_low(m, group):
                wait(pool, a_[f"mh{group}"], m.n + 1)
                wait(pool, a_[f"pv{group}"], m.n)
                g.tensor_tensor(amlo[:, group, :, :], am[:, group, :, :], amhi[:, group, :, :], ALU.subtract)\
                    .then_inc(a_[f"ml{group}"], 1)

            def step(a):
                n0, n1, n2, n3, n4 = a, a.back(1), a.back(2), a.back(3), a.back(4)
                if n0.inside(NC):
                    wait(pool, a_["xn"], n0.n)
                    root(0, a_["mv"], a_["ve"], a_["rs"], n0.n + 1)
                if n3.inside(NC):
                    wait(pool, a_["ahi"], n3.n + 1)
                    wait(pool, a_["aT"], n3.n)
                    g.tensor_tensor(a16[:, 1, :], attn[:, :], a16[:, 0, :], ALU.subtract).then_inc(a_["alo"], 1)
                if n0.inside(NC):
                    if n0.c == 0:
                        wait(pool, s_moda, 16 * (n0.b + 1))
                    wait(pool, a_["xn"], n0.n + 1)
                    modulate(h[:, :], n0, mod_a, "hm", "h")
                if n2.inside(NC):
                    scores_low(n2, 1)
                if n3.inside(NC):
                    wait(pool, a_["t1"], n3.n + 1)
                    g.tensor_tensor(x1[:, n3.p, :], x1[:, n3.p, :], x_slot(n3), ALU.add).then_inc(a_["x1"], 1)
                if n4.inside(NC):
                    if n4.c == 0:
                        wait(pool, s_modb, 16 * (n4.b + 1))
                    wait(pool, a_["xn2"], n4.n + 1)
                    modulate(h2[:, :], n4, mod_b, "hm2", "h2")
                if n0.inside(NC):
                    wait(pool, a_["rope"], n0.n + 1)
                    g.tensor_tensor(ra[:, :], ra[:, :], rb[:, :], ALU.add).then_inc(a_["R"], 1)
                if n1.inside(NC):
                    scores_low(n1, 0)
                if n3.inside(NC):
                    wait(pool, a_["xn2"], n3.n)
                    root(1, a_["mv2"], a_["ve2"], a_["rs2"], n3.n + 1)

            steps_a(pool, step)

            pool.wait_ge(s_row[0], 16 * (NC // 2))
            pool.wait_ge(s_row[1], 16 * (NC // 2))
            pool.wait_ge(s_gb, 16)
            pool.wait_ge(s_out[0], 16 * (NC // 2))
            pool.wait_ge(s_out[1], 16 * (NC // 2))

            def gather(m):
                wait(pool, c_["gi"], m.n + 1)
                wait(pool, c_["yw"], m.n - 3)
                carry(pool)
                g.indirect_dma_start(xg[:, m.c, :], None, rows_d,
                                     bass.IndirectOffsetOnAxis(ap=gi[:, m.c:m.c + 1], axis=0))\
                    .then_inc(s_g[m.c], 16)

            gather(At(0, 0, UC))
            gather(At(0, 1, UC))

            def step_c(a):
                m = a.back(2)
                if m.inside(MAXB):
                    wait(pool, c_["yw"], m.n + 1)
                    wait(pool, s_sc, 16 * m.n)
                    carry(pool)
                    g.indirect_dma_start(out_rows, bass.IndirectOffsetOnAxis(ap=si[:, m.c:m.c + 1], axis=0),
                                         yw[:, m.p, :], None, bounds_check=T - 1, oob_is_err=False,
                                         compute_op=ALU.add).then_inc(s_sc, 16)
                m = a.back(-2)
                if m.inside(MAXB):
                    gather(m)

            steps_c(pool, step_c)
            pool.wait_ge(s_sc, 16 * MAXB)

        @block.scalar
        def _(act):
            v = nc.scalar

            def copy(out_, in_, scale=1.0):
                return v.activation(out_, in_, ACT.Copy, scale=scale)

            act.wait_ge(s_ld["c"], 16)
            v.activation(c_exp, c_raw, ACT.Exp, scale=-1.0).then_inc(s_act, 1)
            act.wait_ge(s_ld["wq"], 16)
            copy(wqhi[:, :, :], wq_raw, WS).then_inc(s_act, 1)
            act.wait_ge(s_ld["wo"], 16)
            copy(wohi[:, :, :], wo_raw, WS).then_inc(s_act, 1)
            act.wait_ge(s_pool, POOL_CONST)

            def scores_high(m, g):
                wait(act, a_[f"m{g}"], m.n + 1)
                wait(act, a_[f"pv{g}"], m.n)
                copy(amhi[:, g, :, :], am[:, g, :, :]).then_inc(a_[f"mh{g}"], 1)

            def step(a):
                n0, n1, n2, n3, n4, n5 = (a.back(k) for k in range(6))
                if n5.inside(NC):
                    wait(act, a_["h2T"], n5.n + 1)
                    wait(act, a_["lg"], n5.n)
                    copy(h2T[:, :, :], bank[0][:, 0:D].bitcast(F16).rearrange("p (q n) -> p q n", q=2))\
                        .then_inc(a_["h2Te"], 1)
                if n0.inside(NC):
                    wait(act, s_w[n0.p], 16 * (n0.pairs + 1))
                    copy(piece(n0, 0), stage[:, n0.p, :], WS).then_inc(a_["whi"], 1)
                if n5.inside(NC):
                    wait(act, a_["lg"], n5.n + 1)
                    copy(logits[:, :, bass.ds(n5.n, 1)],
                         bank[0][:, 0:E].rearrange("p (e u) -> p e u", u=1), 1.0 / WS).then_inc(a_["lge"], 1)
                if n1.inside(NC):
                    wait(act, a_["Tq"], n1.n + 1)
                    wait(act, a_["pv0"], n1.n)
                    copy(qstT[:, :], bank[3][:, :].bitcast(F16)).then_inc(a_["qTs"], 1)
                if n3.inside(NC):
                    wait(act, a_["aT"], n3.n + 1)
                    wait(act, a_["pj"], n3.n)
                    copy(aT[:, :, :], bank[0][:, 0:D].bitcast(F16).rearrange("p (q n) -> p q n", q=2))\
                        .then_inc(a_["aTe"], 1)
                if n0.inside(NC):
                    wait(act, a_["h"], n0.n + 1)
                    wait(act, a_["hT"], n0.n)
                    copy(h16[:, 0, :], h[:, :]).then_inc(a_["hhi"], 1)
                    wait(act, a_["hT"], n0.n + 1)
                    wait(act, a_["qk"], n0.n)
                    copy(hT[:, :, :], bank[0][:, 0:D].bitcast(F16).rearrange("p (q n) -> p q n", q=2))\
                        .then_inc(a_["hTe"], 1)
                    wait(act, a_["v"], n0.n + 1)
                    wait(act, a_["pv1"], n0.n - CPB + 1)
                    copy(v16[:, n0.c, 0, :, 0:HD], bank[2][:, 0:D].rearrange("p (h d) -> p h d", d=HD),
                         1.0 / WS).then_inc(a_["vhi"], 1)
                if n1.inside(NC):
                    scores_high(n1, 0)
                if n4.inside(NC):
                    wait(act, a_["h2"], n4.n + 1)
                    wait(act, s_row[n4.p], 16 * n4.pairs)
                    wait(act, a_["h2T"], n4.n - 1)
                    copy(h2_16[:, n4.p, 0, :], h2[:, :]).then_inc(a_["h2hi"], 1)
                if n1.inside(NC) and n1.c < CPB - 1:
                    k = (CPB - 1) * n1.b + n1.c
                    wait(act, a_["state"], k + 1)
                    wait(act, a_["pv0"], n1.n - 1)
                    copy(own(state[:, n1.p, 0, :], 0), own(bank[4][:, 0:NH * VW], 0))
                    copy(own(state[:, n1.p, 0, :], 1), own(bank[4][:, 0:NH * VW], 1)).then_inc(a_["sth"], 1)
                if n0.inside(NC):
                    wait(act, a_["R"], n0.n + 1)
                    wait(act, a_["slo"], n0.n)
                    v.activation(rb[:, :], ra[:, :], ACT.Relu)
                    v.activation(feat[:, :], ra[:, :], ACT.Exp).then_inc(a_["exp"], 1)
                if n1.inside(NC):
                    scores_high(n1, 1)
                if n0.inside(NC):
                    wait(act, a_["f"], n0.n + 1)
                    wait(act, a_["Tk"], n0.n)
                    k = (CPB - 1) * n0.b + n0.c
                    wait(act, a_["state"], k)
                    f = feat[:, :].rearrange("p (q h u d) -> p q h u d", q=2, h=NH, u=1)
                    copy(qst[:, :, 0:3:2, :], f[:, 0].broadcast_to([P, NH, 2, HD]))
                    copy(kst[:, :, 0:2, :], f[:, 1].broadcast_to([P, NH, 2, HD])).then_inc(a_["shi"], 1)
                if n2.inside(NC):
                    wait(act, a_["at"], n2.n + 1)
                    wait(act, a_["aT"], n2.n)
                    copy(a16[:, 0, :], attn[:, :]).then_inc(a_["ahi"], 1)

            steps_a(act, step)

            act.wait_ge(s_dve, marks["shift"])
            flat = stage[:, :, :].rearrange("p q n -> p (q n)")
            v.activation(flat[:, 0:256], flat[:, 256:512], ACT.Exp).then_inc(s_act, 1)

            def step_c(a):
                if a.inside(MAXB):
                    for g, ready, done, freed in ((0, "hA", "gA", "glA"), (1, "hB", "gB", "glB")):
                        src = bank[3 + 2 * a.p + g][:, :]
                        h_ = slice(g * 512, g * 512 + 512)
                        wait(act, c_[ready], a.n + 1)
                        wait(act, c_[freed], a.n - 1)
                        v.activation(g32[:, a.p, h_], src, ACT.Gelu, scale=1.0 / WS)
                        wait(act, c_["y"], a.n - 1)
                        v.activation(ghi[:, a.p, h_], src, ACT.Gelu, scale=1.0 / WS).then_inc(c_[done], 1)

            steps_c(act, step_c)

        @block.tensor
        def _(pe):
            t = nc.tensor

            def mm3(dst, xhi_, xlo_, whi, wlo, start=True, stop=True):
                t.matmul(dst, xhi_, whi, start=start, stop=False)
                t.matmul(dst, xhi_, wlo, start=False, stop=False)
                return t.matmul(dst, xlo_, whi, start=False, stop=stop)

            pe.wait_ge(s_pool, POOL_CONST)
            pe.wait_ge(s_dve, marks["silu"])
            pe.wait_ge(s_ld["rw"], 16)
            for i, src in enumerate((c_silu, rw_raw)):
                for k in range(KT):
                    o = (i * KT + k) * B
                    last = t.transpose(bank[0][:, o:o + B], src[:, k * P:(k + 1) * P], ident[0:B, 0:B])
            last.then_inc(s_pe, 1)
            pe.wait_ge(s_dve, marks["t"])
            pe.wait_ge(s_ld["wmod"], 16)
            for j in range(3):
                for k in range(KT):
                    last = t.matmul(bank[1 + j][0:B, :], cT[:, k, :], wmod_raw[:, k, 512 * j:512 * j + 512],
                                    start=(k == 0), stop=(k == KT - 1))
            last.then_inc(s_pe, 1)
            pe.wait_ge(s_dve, marks["wo"])

            def scores(g, name):
                for h in range(HG * g, HG * g + HG):
                    j, odd = h // 2, h % 2
                    rows = slice(64 * odd, 64 * odd + 64)
                    cols = slice(j * P, j * P + P)
                    o = (j % 4) * P
                    last = t.matmul(bank[5 + odd][:, o:o + P], kstT[rows, cols], qstT[rows, cols],
                                    start=True, stop=True)
                last.then_inc(a_[name], 1)

            def earlier(m):
                for j in range(NH // 2):
                    two = slice(2 * j * VW, (2 * j + 2) * VW)
                    for i in range(2):
                        t.matmul(bank[7][:, two], qstT[:, j * P:(j + 1) * P], state[:, 1 - m.p, i, two],
                                 start=(j == i == 0), stop=False, skip_group_check=True)

            def attend(m, g):
                wait(pe, a_[f"ml{g}"], m.n + 1)
                for h_ in range(HG * g, HG * g + HG):
                    o = bank[7][:, h_ * VW:(h_ + 1) * VW]
                    q = slice(h_ // 2 % 4 * P, (h_ // 2 % 4 + 1) * P)
                    hi, lo = amhi[:, g, h_ % 2, q], amlo[:, g, h_ % 2, q]
                    vhi, vlo = v16[:, m.c, 0, h_, :], v16[:, m.c, 1, h_, :]
                    t.matmul(o, hi, vhi, start=(m.c == 0), stop=False, skip_group_check=True)
                    t.matmul(o, hi, vlo, start=False, stop=False, skip_group_check=True)
                    last = t.matmul(o, lo, vhi, start=False, stop=True, skip_group_check=True)
                last.then_inc(a_[f"pv{g}"], 1)

            def transpose_parts(dst, src, n=2 * KT):
                for j in range(n):
                    last = t.transpose(dst[:, :].bitcast(F16)[:, j * P:(j + 1) * P], src[:, j * P:(j + 1) * P],
                                       ident16[:, :])
                return last

            def flat3(t_):
                return t_.rearrange("p q n -> p (q n)")

            def flat4(t_):
                return t_.rearrange("p h c d -> p (h c d)")

            def product(dst, xT_, whi, wlo, n):
                for k in range(KT):
                    c_k = slice(k * P, (k + 1) * P)
                    last = mm3(dst, xT_[:, 0, c_k], xT_[:, 1, c_k], whi[:, k, n], wlo[:, k, n],
                               start=(k == 0), stop=(k == KT - 1))
                return last

            def bank_free(a, *users):
                for name, back in users:
                    m = a.back(back)
                    if m.inside(NC):
                        wait(pe, a_[name], m.n + 1)
                        return

            def step(a):
                n0, n1, n2, n3, n4, n5 = (a.back(k) for k in range(6))
                if n5.inside(NC):
                    wait(pe, a_["h2Te"], n5.n + 1)
                    product(bank[0][:, 0:E], h2T, rwhi, rwlo, slice(0, E)).then_inc(a_["lg"], 1)
                if n1.inside(NC):
                    wait(pe, a_["slo"], n1.n + 1)
                    wait(pe, a_["kTs"], n1.n)
                    transpose_parts(bank[3], flat4(qst[:, :, :, :]), 8).then_inc(a_["Tq"], 1)
                if n3.inside(NC):
                    wait(pe, a_["alo"], n3.n + 1)
                    bank_free(a, ("lge", 5), ("h2Te", 5), ("hTe", 1), ("aTe", 4))
                    transpose_parts(bank[0], flat3(a16[:, :, :])).then_inc(a_["aT"], 1)
                if n1.inside(NC):
                    wait(pe, a_["qTs"], n1.n + 1)
                    transpose_parts(bank[3], flat4(kst[:, :, :, :]), 8).then_inc(a_["Tk"], 1)
                if n3.inside(NC):
                    wait(pe, a_["aTe"], n3.n + 1)
                    bank_free(a, ("vlo", 1), ("t1", 4))
                    product(bank[2][:, 0:D], aT, wohi, wolo, slice(0, D)).then_inc(a_["pj"], 1)
                if n0.inside(NC):
                    wait(pe, a_["hlo"], n0.n + 1)
                    bank_free(a, ("aTe", 3), ("hTe", 1))
                    transpose_parts(bank[0], flat3(h16[:, :, :])).then_inc(a_["hT"], 1)
                if n1.inside(NC):
                    wait(pe, a_["kTs"], n1.n + 1)
                    wait(pe, a_["m1"], n1.n)
                    scores(0, "sc0")
                if n0.inside(NC):
                    wait(pe, a_["hTe"], n0.n + 1)
                    bank_free(a, ("t1", 3), ("vlo", 1))
                    product(bank[2][:, 0:D], hT, wqhi, wqlo, slice(2 * D, 3 * D)).then_inc(a_["v"], 1)
                    wait(pe, a_["rope"], n0.n)
                    product(bank[1][:, :], hT, wqhi, wqlo, slice(0, 2 * D)).then_inc(a_["qk"], 1)
                if n1.inside(NC) and n1.c < CPB - 1:
                    wait(pe, a_["vlo"], n1.n + 1)
                    wait(pe, a_["stl"], (CPB - 1) * n1.b + n1.c)
                    for j in range(NH // 2):
                        two = slice(2 * j, 2 * j + 2)
                        o = bank[4][:, two.start * VW:two.stop * VW]
                        k_ = kst[:, two, :, :].rearrange("p h c d -> p (h c d)")
                        for i in range(2):
                            last = t.matmul(o, k_, v16[:, n1.c, i, two, :].rearrange("p h w -> p (h w)"),
                                            start=(n1.c == j == i == 0), stop=(i == 1), skip_group_check=True)
                    last.then_inc(a_["state"], 1)
                if n1.inside(NC):
                    wait(pe, a_["m0"], n1.n + 1)
                    scores(1, "sc1")
                if n2.inside(NC):
                    attend(n2, 1)
                if n4.inside(NC):
                    wait(pe, a_["h2lo"], n4.n + 1)
                    bank_free(a, ("hTe", 0), ("aTe", 3), ("lge", 5))
                    transpose_parts(bank[0], flat3(h2_16[:, n4.p, :, :])).then_inc(a_["h2T"], 1)
                if n1.inside(NC):
                    wait(pe, a_["at"], n1.n)
                    if n1.c > 0:
                        wait(pe, a_["stl"], (CPB - 1) * n1.b + n1.c)
                        earlier(n1)
                    attend(n1, 0)

            steps_a(pe, step)

            flat = stage[:, :, :].rearrange("p q n -> p (q n)")
            sel = flat[:, 5 * 256:5 * 256 + 128].bitcast(F16)
            pe.wait_ge(s_dve, marks["sel"])
            t.matmul(bank[1][:, 0:E * NC], before[:, :], sel, start=True, stop=True)
            t.matmul(bank[2][:, 0:E * NC], ones[:, :], sel, start=True, stop=True).then_inc(s_pe, 1)

            def pair(i, n, first=False, final=False):
                for k in range(2):
                    wait(pe, b_["a"], n * 2 + k + 1)
                    last = t.matmul(bank[7][:, 0:2 * TB], b_one[:, k, :],
                                    b_rhs[:, k, :, :].rearrange("p q j -> p (q j)"),
                                    start=(first and k == 0), stop=(final and k == 1))
                    last.then_inc(b_["mm"], 1)

            pair(0, 0, first=True)
            with pe.Fori(1, NC - 1) as i:
                pair(i, i)
            pair(NC - 1, NC - 1, final=True)
            pe.wait_ge(b_["mm"], 2 * NC)
            pe.sem_inc(s_pe, 1)

            def xT(m):
                wait(pe, s_g[m.c], 16 * (m.b + 1))
                wait(pe, c_["xTe"], m.n - 1)
                transpose_parts(bank[7 * m.p], xg[:, m.c, 0:D].bitcast(F16)).then_inc(c_["xT"], 1)

            pe.wait_ge(s_dve, marks["block_e"])
            pe.wait_ge(a_["whi"], NC)
            pe.wait_ge(a_["wlo"], NC)
            xT(At(0, 0, UC))

            expert = {}

            def step_c(a):
                if a.c == 0 and a.inside(MAXB):
                    five = pe.value_load(block_e[0:1, bass.ds(a.b, 1)], min_val=0, max_val=E ** (UC + 1) - 1)
                    for c in (*range(UC), -1):
                        expert[c] = five % E
                        five = five // E
                if a.back(-1).inside(MAXB):
                    xT(a.back(-1))
                if a.inside(MAXB):
                    e = expert[a.c]
                    wait(pe, c_["xTe"], a.n + 1)
                    for mt in range(MT):
                        g, q = mt // 4, mt % 4
                        if q == 0:
                            wait(pe, c_["gA" if g == 0 else "gB"], a.n - 1)
                        dst = bank[3 + 2 * a.p + g][:, q * P:(q + 1) * P]
                        for k in range(KT):
                            w_ = bass.ds(e * EW + (k * H + mt * P), P)
                            c_k = slice(k * P, (k + 1) * P)
                            last = mm3w(dst, w1hi[:, w_], w1lo[:, w_], x16[:, a.p, c_k], x16[:, a.p, D:2 * D][:, c_k],
                                        start=(k == 0), stop=(k == KT - 1))
                        if q == 3:
                            last.then_inc(c_["hA" if g == 0 else "hB"], 1)
                m = a.back(1)
                if m.inside(MAXB):
                    e = expert[a.c - 1]
                    wait(pe, c_["yw"], m.n - 1)
                    for mt in range(MT):
                        if mt % 4 == 0:
                            wait(pe, c_["glA" if mt == 0 else "glB"], m.n + 1)
                        w_ = bass.ds(e * EW + mt * D, D)
                        c_m = slice(mt * P, (mt + 1) * P)
                        last = mm3(bank[1 + m.p][:, 0:D], ghi[:, m.p, c_m], glo[:, m.p, c_m], w2hi[:, w_], w2lo[:, w_],
                                   start=(mt == 0), stop=(mt == MT - 1))
                    last.then_inc(c_["y"], 1)

            def mm3w(dst, whi, wlo, xhi_, xlo_, start, stop):
                t.matmul(dst, whi, xhi_, start=start, stop=False)
                t.matmul(dst, whi, xlo_, start=False, stop=False)
                return t.matmul(dst, wlo, xhi_, start=False, stop=stop)

            steps_c(pe, step_c)

        @block.sync
        def _(sp):
            def load_x(a):
                wait(sp, a_["xn"], a.n - CPB + 1)
                carry(sp)
                sp.dma_start(x_slot(a), x_rows[bass.ds(a.n * P, P), :]).then_inc(s_x[a.c], 16)

            def load_mod(dst, b, lo, done):
                sp.dma_start(dst[:, :], mod_d[bass.ds(b, 1), lo * D:lo * D + dst.shape[1]].broadcast_to(
                    [P, dst.shape[1]])).then_inc(done, 16)

            def load_piece(a):
                wait(sp, a_["wlo"], a.n - 1)
                if a.c < KT:
                    src = w1_v[:, bass.ds(a.b, 1), a.c, :].rearrange("p e h -> p (e h)")
                    dst = stage[:, a.p, :]
                else:
                    q = MT // 2
                    src = w2_v[:, bass.ds(a.b, 1), (a.c - KT) * q:(a.c - KT + 1) * q, :].rearrange(
                        "p e m d -> p (e m) d")
                    dst = stage[:, a.p, :].rearrange("p (m d) -> p m d", m=q)
                carry(sp)
                sp.dma_start(dst, src).then_inc(s_w[a.p], 16)

            sp.dma_start(c_raw, c_in).then_inc(s_ld["c"], 16)
            sp.dma_start(wmod_raw, wmod.rearrange("(k p) n -> p k n", p=P)).then_inc(s_ld["wmod"], 16)
            sp.dma_start(rw_raw, router_w).then_inc(s_ld["rw"], 16)
            load_x(At(0, 0, CPB))
            load_x(At(0, 1, CPB))
            sp.dma_start(wq_raw, w_qkv.rearrange("(k p) n -> p k n", p=P)).then_inc(s_ld["wq"], 16)
            sp.dma_start(cos_t[:, :, :], rope_cos).then_inc(s_ld["cos"], 16)
            sp.dma_start(sin_t[:, :, :, :], rope_sin).then_inc(s_ld["sin"], 16)
            sp.dma_start(wo_raw, w_out.rearrange("(k p) n -> p k n", p=P)).then_inc(s_ld["wo"], 16)
            sp.wait_ge(s_dve, marks["mod"])
            sp.dma_start(mod_d, mod_s).then_inc(s_ms, 16)
            sp.wait_ge(s_ms, 16)
            load_mod(mod_a, 0, 0, s_moda)
            load_mod(mod_g, 0, 2, s_modg)
            load_mod(mod_b, 0, 3, s_modb)
            load_piece(At(0, 0, CPB))
            sp.dma_start(rows_d.rearrange("(b s) n -> b s n", b=B)[:, :, D:2 * D],
                         mod_d[:, MOD["gb"]:MOD["gb"] + D].rearrange("b (u d) -> b u d", u=1).broadcast_to([B, S, D]))\
                .then_inc(s_gb, 16)

            def step(a):
                n3, n4 = a.back(3), a.back(4)
                first = isinstance(a.b, int) and a.n < 2 * CPB
                if a.c == 0 and a.inside(NC) and not (first and a.b == 0):
                    wait(sp, a_["h"], a.n)
                    carry(sp)
                    load_mod(mod_a, a.b, 0, s_moda)
                if n3.c == 0 and n3.inside(NC) and not (first and n3.n == 0):
                    wait(sp, a_["t1"], n3.n)
                    carry(sp)
                    load_mod(mod_g, n3.b, 2, s_modg)
                if n4.c == 0 and n4.inside(NC) and not (first and n4.n == 0):
                    wait(sp, a_["h2"], n4.n)
                    carry(sp)
                    load_mod(mod_b, n4.b, 3, s_modb)
                if a.back(-1).inside(NC):
                    load_piece(a.back(-1))
                if a.back(-2).inside(NC):
                    load_x(a.back(-2))
                if n3.inside(NC):
                    wait(sp, a_["x1"], n3.n + 1)
                    carry(sp)
                    sp.dma_start(out_rows[bass.ds(n3.n * P, P), :], x1[:, n3.p, :]).then_inc(s_out[n3.p], 16)
                if n4.inside(NC):
                    wait(sp, a_["h2lo"], n4.n + 1)
                    carry(sp)
                    sp.dma_start(rows_d[bass.ds(n4.n * P, P), 0:D],
                                 h2_16[:, n4.p, :, :].rearrange("p q n -> p (q n)").bitcast(F32))\
                        .then_inc(s_row[n4.p], 16)

            steps_a(sp, step)


_INS = ["L0_attn_x", "L0_attn_w_qkv", "L0_attn_w_out", "L0_ffn_router_w", "L0_ffn_w1", "L0_ffn_w2",
        "L0_c", "L0_wmod"]


def rope_tables():
    hd2 = HD // 2
    inv = (np.float32(1.0) / np.float32(10000.0) ** (np.arange(hd2, dtype=np.float32) / np.float32(hd2)))
    ang = np.arange(S, dtype=np.float32)[:, None] * inv.astype(np.float32)[None, :]
    scale = np.float32(Q_SCALE / WS)
    cos, sin = np.cos(ang) * scale, np.sin(ang) * scale
    by_place = lambda t: np.ascontiguousarray(
        t.reshape((CPB, P) + t.shape[1:]).swapaxes(0, 1), dtype=np.float32)
    return by_place(cos), by_place(np.stack([-sin, sin], axis=1))


def kernel(**inputs):
    import concourse.bacc as _bacc
    from concourse.bass_utils import run_bass_kernel_spmd as _run

    nc = _bacc.Bacc("TRN2", target_bir_lowering=False, num_devices=1)
    arrays = {f"in_{name}_dram": np.ascontiguousarray(inputs[name]) for name in _INS}
    arrays["rope_cos"], arrays["rope_sin"] = rope_tables()
    args = [nc.dram_tensor(name, a.shape, mybir.dt.from_np(a.dtype), kind="ExternalInput").ap()
            for name, a in arrays.items()]
    args.append(nc.dram_tensor("out_dram", (B, S, D), F32, kind="ExternalOutput").ap())
    adaln_block(nc, *args)
    r = _run(nc, [arrays], core_ids=[0])
    return r.results[0]["out_dram"]
```

```python
from contextlib import ExitStack

import numpy as np

import concourse.bass as bass
from concourse import mybir

ALU = mybir.AluOpType
ACT = mybir.ActivationFunctionType
AX_X = mybir.AxisListType.X
F32 = mybir.dt.float32
F16 = mybir.dt.float16
I32 = mybir.dt.int32
U32 = mybir.dt.uint32

P = 128
B, S, D = 8, 512, 256
NH, HD = 16, 16
E, H = 8, 1024
KT = D // P
MT = H // P
CPB = S // P
NC = B * CPB
T = B * S
VW = HD + 1
HG = 8
EW = KT * H
PIECE = 2 * EW // CPB
MAXB = (2 * T + E * (P - 1)) // P
UC = 8
TB = -(-MAXB // UC) * UC
LN_EPS = 1e-5
DEN_MIN = 1e-6
TOP_EPS = 1e-9
GATE_MIN = 0.25
WS = 64.0
Q_SCALE = float(HD ** -0.25)
LAG_A = 5
ORDER_PE = (("pv1", 3), ("h2T", 5), ("earlier", 2), ("state", 1), ("hT", 0), ("Tq", 1), ("qk", 0), ("v", 0),
            ("Tk", 1), ("pv0", 2), ("aT", 3), ("sc0", 1), ("pj", 3), ("lg", 5), ("sc1", 1))
ORDER_DVE = (("t1", 4), ("stats", 0), ("mv", 0), ("den", 3), ("xc", 0), ("at", 3), ("h", 0), ("sloq", 1),
             ("m1", 2), ("stl", 1), ("stats2", 4), ("mv2", 4), ("xc2", 4), ("wlo2", 1), ("rope", 0),
             ("kTs", 1), ("vlo", 0), ("h2", 4), ("wlo", 0), ("m0", 1), ("f", 0))
ORDER_POOL = (("x1", 4), ("rs", 0), ("slok", 1), ("hlo", 0), ("ml0", 2), ("alo", 3), ("rs2", 4), ("R", 0),
              ("ml1", 2), ("h2lo", 4))
ORDER_ACT = (("shi", 1), ("mh0", 2), ("ahi", 3), ("hhi", 0), ("h2Te", 5), ("sth", 1), ("hTe", 0), ("qTs", 1),
             ("mh1", 2), ("whi", 0), ("vhi", 0), ("aTe", 3), ("exp", 0), ("h2hi", 4), ("lge", 5))
LAG_C = 2
NOWHERE = 2 * T
GB = 4


class At:

    def __init__(self, b, c, unroll):
        self.unroll, self.b, self.c = unroll, b + c // unroll, c % unroll
        self.n = self.b * unroll + self.c
        self.p = self.c % 2
        self.pairs = self.b * (unroll // 2) + self.c // 2

    def slot(self, count):
        return self.c % count, self.b * (self.unroll // count) + self.c // count

    def back(self, k):
        return At(self.b, self.c - k, self.unroll)

    def inside(self, count):
        return not isinstance(self.n, int) or 0 <= self.n < count


def wait(eng, sem, value, most=None):
    if isinstance(value, int):
        if most is not None:
            value = min(value, most)
        if value <= 0:
            return
    eng.wait_ge(sem, value)


def adaln_block(nc, x, w_qkv, w_out, router_w, w1, w2, c_in, wmod, rope_cos, rope_sin, out):
    ctx = ExitStack()
    with ctx:
        def sb(name, shape, dt=F32):
            return ctx.enter_context(nc.sbuf_tensor(name, shape, dt))

        def sem(name):
            return ctx.enter_context(nc.semaphore(name))

        bank = [ctx.enter_context(nc.psum_tensor(f"bank{i}", [P, 512], F32)) for i in range(8)]
        mod_d = nc.dram_tensor("mod_rows", (B, 6 * D), F32, kind="Internal").ap()
        rows_d = nc.dram_tensor("ffn_rows", (T, 2 * D), F32, kind="Internal").ap()

        w1hi = sb("w1hi", [P, E * EW], F16)
        w1lo = sb("w1lo", [P, E * EW], F16)
        w2hi = sb("w2hi", [P, E * EW], F16)
        w2lo = sb("w2lo", [P, E * EW], F16)
        stage = sb("stage", [P, 2, PIECE])

        ident16 = sb("ident16", [P, P], F16)
        causal = sb("causal", [P, P])
        before = sb("before", [P, P], F16)
        ones = sb("ones", [P, P], F16)
        consts = sb("consts", [P, 2])
        eps, minus_half = consts[:, 0:1], consts[:, 1:2]
        cos_t = sb("cos_t", [P, CPB, HD // 2])
        sin_t = sb("sin_t", [P, CPB, 2, HD // 2])
        wqhi = sb("wqhi", [P, KT, 3 * D], F16)
        wqlo = sb("wqlo", [P, KT, 3 * D], F16)
        wohi = sb("wohi", [P, KT, D], F16)
        wolo = sb("wolo", [P, KT, D], F16)
        rwhi = sb("rwhi", [P, KT, E], F16)
        rwlo = sb("rwlo", [P, KT, E], F16)
        mod_a = sb("mod_a", [P, 2 * D])
        mod_g = sb("mod_g", [P, D])
        mod_b = sb("mod_b", [P, 2 * D])
        logits = sb("logits", [P, E, NC])

        xt = sb("xt", [P, 2 * CPB * D])
        st = sb("st", [P, 2, 6])
        mv = sb("mv", [P, 2, 2])
        var = sb("var", [P, 2])
        rstd = sb("rstd", [P, 2])
        h16 = sb("h16", [P, 2, D], F16)
        hT = sb("hT", [P, 2, D], F16)
        ra = sb("ra", [P, 2 * D])
        rb = sb("rb", [P, 2 * D])
        h = rb[:, 0:D]
        feat = sb("feat", [P, 2 * D])
        v16 = sb("v16", [P, CPB, 2, NH, VW], F16)
        qst = sb("qst", [P, NH, 4, HD], F16)
        kst = sb("kst", [P, NH, 4, HD], F16)
        qstT = sb("qstT", [P, 8 * P], F16)
        kstT = sb("kstT", [P, 8 * P], F16)
        am = sb("am", [P, 2, 2, 4 * P])
        amhi = sb("amhi", [P, 2, 2, 4 * P], F16)
        amlo = sb("amlo", [P, 2, 2, 4 * P], F16)
        state = sb("state", [P, 2, 2, NH * VW], F16)
        den = sb("den", [P, 2, NH])
        attn = ra[:, 0:D]
        a16 = sb("a16", [P, 2, D], F16)
        aT = sb("aT", [P, 2, D], F16)
        x1 = sb("x1", [P, 2, D])
        h2 = sb("h2", [P, D])
        h2_16 = sb("h2_16", [P, 2, 2, D], F16)
        h2T = sb("h2T", [P, 2, D], F16)

        iota_f = sb("iota_f", [P, P])
        tile_f = sb("tile_f", [P, NC])
        id1 = sb("id1", [P, NC])
        small = feat[:, 0:14 * NC].rearrange("p (k i) -> p k i", k=14)
        slot_i = ra[:, 0:4 * NC].bitcast(I32).rearrange("p (u k i) -> p u k i", u=2, k=2)
        slot_f = ra[:, 4 * NC:8 * NC].rearrange("p (u k i) -> p u k i", u=2, k=2)
        w_q = wqlo[:, :, :].rearrange("p k n -> p (k n)").bitcast(F32)
        block_e, gidx, sidx, cwT = (w_q[:, i * TB:(i + 1) * TB] for i in range(4))
        block_e, gidx, sidx = (t.bitcast(I32) for t in (block_e, gidx, sidx))
        gi = sb("gi", [P, GB], U32)
        si = sb("si", [P, GB], U32)

        def halves(t):
            return t.rearrange("p (q n) -> p q n", q=2)

        xg = xt[:, :].rearrange("p (q n) -> p q n", q=GB)
        g32 = am[:, :, :, :].rearrange("p g o n -> p g (o n)")
        ghi = halves(amhi[:, :, :, :].rearrange("p g o n -> p (g o n)"))
        glo = halves(amlo[:, :, :, :].rearrange("p g o n -> p (g o n)"))
        x16 = qstT[:, :].rearrange("p (q n) -> p q n", q=2)
        yw = x1
        b_place = am[:, :, :, :].rearrange("p g o n -> p (g o n)")[:, 0:2 * 4 * P].rearrange(
            "p (w k i t) -> p w k i t", w=2, k=2, i=2)
        b_block = amhi[:, :, :, :].rearrange("p g o n -> p (g o n)").bitcast(F32)[:, 0:2 * 4 * TB].rearrange(
            "p (w k i j) -> p w k i j", w=2, k=2, i=2)
        b_rhs = xt[:, 0:2 * 8 * TB].rearrange("p (w k i q j) -> p w k i q j", w=2, k=2, i=2, q=2)
        w_ones = rb[:, 0:E * NC]
        rev = sb("rev", [P, E])

        half = E // 2 * EW
        late = [t[:, half:2 * half].bitcast(F32) for t in (w2hi, w2lo, w1lo)]
        wmod_raw = late[0][:, 0:KT * 6 * D].rearrange("p (k n) -> p k n", k=KT)
        wq_raw = late[1][:, 0:KT * 3 * D].rearrange("p (k n) -> p k n", k=KT)
        wo_raw = late[1][:, 1536:1536 + KT * D].rearrange("p (k n) -> p k n", k=KT)
        rw_raw = late[1][0:E, 2048:2048 + D]
        ident = late[2][:, 2048:2048 + P]
        iota_i = late[2][:, 2048 + P:2048 + 2 * P].bitcast(I32)
        tile_i = late[2][:, 2048 + 2 * P:2048 + 2 * P + NC].bitcast(I32)
        c_raw = late[1][0:B, 2304:2304 + D]
        c_exp = late[1][0:B, 2560:2560 + D]
        c_silu = late[1][0:B, 2816:2816 + D]
        cT = late[1][:, 3072:3072 + KT * B].rearrange("p (k b) -> p k b", k=KT)
        mod_s = late[2][0:B, 0:6 * D]
        gate_s = late[2][0:B, 1536:1536 + D]
        gate_a = late[2][0:B, 1792:1792 + D]

        def counters(prefix, names):
            return {k: sem(prefix + k) for k in names.split()}

        a_ = counters("a_", "st mv ve rs xc h hhi hlo hT hTe v vhi vlo qk rope R exp f shi sloq slok Tq qTs Tk kTs"
                            " state sth stl ear sc0 m0 mh0 ml0 sc1 m1 mh1 ml1 pv0 pv1 den rec at ahi alo aT aTe pj"
                            " t1 x1 st2 mv2 ve2 rs2 xc2 h2 h2hi h2lo h2T h2Te lg lge whi wlo wlo2")
        s_x = [sem(f"s_x{c}") for c in range(CPB)]
        s_moda = sem("s_moda")
        s_modb = sem("s_modb")
        s_modg = sem("s_modg")
        s_gb = sem("s_gb")
        s_w = [sem("s_w0"), sem("s_w1")]
        s_out = [sem("s_out0"), sem("s_out1")]
        s_row = [sem("s_row0"), sem("s_row1")]
        s_ld = {k: sem("s_ld_" + k) for k in ("c", "wmod", "wq", "wo", "rw", "cos", "sin")}
        s_pool = sem("s_pool")
        s_dve = sem("s_dve")
        s_pe = sem("s_pe")
        s_act = sem("s_act")
        s_ms = sem("s_ms")
        b_ = counters("b_", "block place rhs mm")
        s_carry = sem("s_carry")
        c_ = counters("c_", "gi xT xTe hA hB gA gB glA glB y yw")
        s_g = [sem(f"s_g{q}") for q in range(GB)]
        s_sc = sem("s_sc")

        x_rows = x.rearrange("b s d -> (b s) d")
        out_rows = out.rearrange("b s d -> (b s) d")
        w1_v = w1.rearrange("e (k p) h -> p e k h", p=P)
        w2_v = w2.rearrange("e (m p) d -> p e m d", p=P)
        MOD = {k: i * D for i, k in enumerate(("sa", "ca", "ga", "sb", "cb", "gb"))}

        def x_slot(a):
            return xt[:, bass.ds((a.b % 2) * (CPB * D) + a.c * D, D)]

        def own(t, u):
            return t.rearrange("p (j u w) -> p j u w", u=2, w=VW)[64 * u:64 * u + 64, :, u, :]

        def steps_of(order, works):
            def step(a):
                for name, back in order:
                    m = a.back(back)
                    if m.inside(NC):
                        works[name](m)
            return step

        def steps_a(eng, step, after_first=None):
            for c in range(2 * CPB):
                step(At(0, c, CPB))
                if c == 0 and after_first:
                    after_first()
            with eng.Fori(2, B - 1) as b:
                for c in range(CPB):
                    step(At(b, c, CPB))
            for c in range(CPB + LAG_A):
                step(At(B - 1, c, CPB))

        def steps_b(eng, step):
            for c in range(2):
                step(At(0, c, 2))
            with eng.Fori(1, NC // 4 - 1) as b:
                for c in range(2):
                    step(At(b, c, 2))
            for c in range(2):
                step(At(NC // 4 - 1, c, 2))

        def steps_c(eng, step):
            for c in range(UC):
                step(At(0, c, UC))
            with eng.Fori(1, MAXB // UC) as b:
                for c in range(UC):
                    step(At(b, c, UC))
            for c in range(MAXB % UC + LAG_C):
                step(At(MAXB // UC, c, UC))

        class Chain:

            def __init__(self, eng, sem_):
                self.eng, self.sem, self.n = eng, sem_, 0

            def __call__(self, ins):
                self.n += 1
                ins.then_inc(self.sem, 1)
                self.eng.wait_ge(self.sem, self.n)

        def piece(a, part, half=None):
            t = (w1hi, w1lo, w2hi, w2lo)[2 * (a.c // KT) + part]
            n = PIECE if half is None else PIECE // 2
            return t[:, bass.ds(a.b * EW + (a.c % KT) * PIECE + (half or 0) * n, n)]

        block = ctx.enter_context(nc.Block())

        marks = {}

        def carry(eng):
            eng.sem_inc(s_carry, 1)

        POOL_CONST = 16
        ACT_EXP, ACT_W, ACT_EXP2 = 1, 3, 4
        MOD_BANK = (1, 5, 6)
        PE_T, PE_MOD_A, PE_MOD, PE_RANK, PE_TABLE = 1, 2, 3, 4, 5

        @block.vector
        def _(dve):
            link = Chain(dve, s_dve)
            v = nc.vector

            dve.wait_ge(s_act, ACT_EXP)
            link(v.tensor_scalar(c_exp, c_exp, 1.0, None, ALU.add))
            link(v.reciprocal(c_exp, c_exp))
            link(v.tensor_tensor(c_silu, c_raw, c_exp, ALU.mult))
            marks["silu"] = link.n
            dve.wait_ge(s_pe, PE_T)
            link(v.tensor_copy(cT, bank[0][:, 0:KT * B].rearrange("p (k b) -> p k b", k=KT)))
            rw_ps = bank[0][:, KT * B:KT * (B + E)].rearrange("p (k e) -> p k e", k=KT)
            link(v.tensor_scalar(rwhi[:, :, :], rw_ps, WS, None, ALU.mult))
            link(v.scalar_tensor_tensor(out=rwlo[:, :, :], in0=rw_ps, scalar=WS, in1=rwhi[:, :, :],
                                        op0=ALU.mult, op1=ALU.subtract))
            marks["t"] = link.n
            def modulation(rows):
                for k, add in rows:
                    o = MOD[k]
                    src, dst = bank[MOD_BANK[o // 512]][0:B, o % 512:o % 512 + D], mod_s[:, o:o + D]
                    if add is None:
                        link(v.tensor_scalar(gate_s, src, 0.0, 2.0, ALU.is_ge, ALU.mult))
                        link(v.tensor_copy(gate_a, src))
                        link(v.scalar_tensor_tensor(out=gate_a, in0=gate_a, scalar=-1.0, in1=gate_a,
                                                    op0=ALU.mult, op1=ALU.max))
                        link(v.tensor_scalar(gate_a, gate_a, GATE_MIN, None, ALU.max))
                        link(v.scalar_tensor_tensor(out=dst, in0=gate_s, scalar=-1.0, in1=gate_a,
                                                    op0=ALU.add, op1=ALU.mult))
                    else:
                        link(v.tensor_scalar(dst, src, add, None, ALU.add))

            dve.wait_ge(s_pe, PE_MOD_A)
            modulation((("sa", 0.0), ("ca", 1.0)))
            marks["mod_a"] = link.n
            dve.wait_ge(s_act, ACT_W)
            for raw, hi, lo in ((wq_raw, wqhi, wqlo), (wo_raw, wohi, wolo)):
                link(v.scalar_tensor_tensor(out=lo[:, :, :], in0=raw, scalar=WS, in1=hi[:, :, :],
                                            op0=ALU.mult, op1=ALU.subtract))
            marks["wo"] = link.n
            dve.wait_ge(s_pool, POOL_CONST)
            def stats(src, k, done):
                v.bn_stats(st[:, k, :], src).then_inc(a_[done], 1)

            def mean_var(m, k, ready, free, done):
                wait(dve, a_[ready], m.n + 1)
                wait(dve, a_[free], m.n)
                carry(dve)
                v.bn_aggr(mv[:, k, :], st[:, k, :]).then_inc(a_[done], 1)

            def centred(src, k, dst, rows, done):
                v.scalar_tensor_tensor(out=dst, in0=src, scalar=mv[:, k, 0:1], in1=rows[:, D:2 * D],
                                       op0=ALU.subtract, op1=ALU.mult).then_inc(a_[done], 1)

            def modulated(m, k, dst, rows, centre, ready, done):
                wait(dve, a_[centre], m.n + 1)
                wait(dve, a_[ready], m.n + 1)
                v.scalar_tensor_tensor(out=dst, in0=dst, scalar=rstd[:, k:k + 1], in1=rows[:, 0:D],
                                       op0=ALU.mult, op1=ALU.add).then_inc(a_[done], 1)

            def low(dst, src, high, done):
                v.tensor_tensor(dst, src, high, ALU.subtract).then_inc(a_[done], 1)

            def first_stats(m):
                wait(dve, s_x[m.c], 16 * (m.b + 1))
                stats(x_slot(m), 0, "st")

            def first_centre(m):
                wait(dve, a_["mv"], m.n + 1)
                wait(dve, a_["hlo"], m.n)
                wait(dve, a_["f"], m.n)
                if m.c == 0:
                    wait(dve, s_moda, 16 * (m.b + 1))
                centred(x_slot(m), 0, h[:, :], mod_a, "xc")

            def first_modulated(m):
                modulated(m, 0, h[:, :], mod_a, "xc", "rs", "h")
                if isinstance(m.n, int) and m.n == 0:
                    dve.wait_ge(s_pe, PE_MOD)
                    modulation((("ga", None), ("sb", 0.0), ("cb", 1.0), ("gb", None)))
                    marks["mod"] = link.n

            def v_low(m):
                wait(dve, a_["vhi"], m.n + 1)
                v.scalar_tensor_tensor(out=v16[:, m.c, 1, :, 0:HD],
                                       in0=bank[2][:, 0:D].rearrange("p (h d) -> p h d", d=HD), scalar=1.0 / WS,
                                       in1=v16[:, m.c, 0, :, 0:HD], op0=ALU.mult, op1=ALU.subtract)\
                    .then_inc(a_["vlo"], 1)

            def rope(m):
                wait(dve, a_["qk"], m.n + 1)
                wait(dve, a_["exp"], m.n)
                wait(dve, a_["alo"], m.n - 2)
                half_d = HD // 2
                qk = bank[1][:, :].rearrange("p (h o d) -> p h o d", o=2, d=half_d)
                rbv = rb[:, :].rearrange("p (h o d) -> p h o d", o=2, d=half_d)
                v.tensor_tensor(ra[:, :].rearrange("p (h d) -> p h d", d=half_d),
                                bank[1][:, :].rearrange("p (h d) -> p h d", d=half_d),
                                cos_t[:, m.c:m.c + 1, :].broadcast_to([P, 4 * NH, half_d]), ALU.mult)
                for o in range(2):
                    last = v.tensor_tensor(rbv[:, :, o, :], qk[:, :, 1 - o, :],
                                           sin_t[:, m.c, o:o + 1, :].broadcast_to([P, 2 * NH, half_d]), ALU.mult)
                last.then_inc(a_["rope"], 1)

            def features(m):
                wait(dve, a_["exp"], m.n + 1)
                v.scalar_tensor_tensor(out=feat[:, :], in0=feat[:, :], scalar=1.0, in1=rb[:, :],
                                       op0=ALU.min, op1=ALU.add).then_inc(a_["f"], 1)

            def q_low(m):
                wait(dve, a_["shi"], m.n + 1)
                f = feat[:, 0:D].rearrange("p (h u d) -> p h u d", h=NH, u=1)
                low(qst[:, :, 1:4:2, :], f.broadcast_to([P, NH, 2, HD]), qst[:, :, 0:3:2, :], "sloq")

            def k_copy(m):
                wait(dve, a_["Tk"], m.n + 1)
                wait(dve, a_["sc1"], m.n)
                v.tensor_copy(kstT[:, :], bank[6][:, :].bitcast(F16)).then_inc(a_["kTs"], 1)

            def mask(m, g):
                wait(dve, a_[f"sc{g}"], m.n + 1)
                wait(dve, a_[f"ml{g}"], m.n)
                for odd in range(2):
                    last = v.tensor_tensor(am[:, g, odd, :].rearrange("p (h t) -> p h t", t=P),
                                           bank[5 + odd][:, :].rearrange("p (h t) -> p h t", t=P),
                                           causal[:, :].rearrange("p (u t) -> p u t", u=1).broadcast_to([P, 4, P]),
                                           ALU.mult)
                last.then_inc(a_[f"m{g}"], 1)

            def state_low(m):
                if m.c == CPB - 1:
                    return
                wait(dve, a_["sth"], (CPB - 1) * m.b + m.c + 1)
                v.tensor_tensor(own(state[:, m.p, 1, :], 0), own(bank[4][:, 0:NH * VW], 0),
                                own(state[:, m.p, 0, :], 0), ALU.subtract)
                low(own(state[:, m.p, 1, :], 1), own(bank[4][:, 0:NH * VW], 1), own(state[:, m.p, 0, :], 1), "stl")

            sums = bank[7][:, 0:NH * VW].rearrange("p (h w) -> p h w", w=VW)

            def denominator(m):
                wait(dve, a_["pv1"], m.n + 1)
                v.tensor_scalar(den[:, 0, :], sums[:, :, HD], DEN_MIN, None, ALU.max).then_inc(a_["den"], 1)

            def quotient(m):
                wait(dve, a_["den"], m.n + 1)
                v.reciprocal(den[:, 1, :], den[:, 0, :]).then_inc(a_["rec"], 1)
                wait(dve, a_["rec"], m.n + 1)
                wait(dve, a_["alo"], m.n)
                wait(dve, a_["exp"], m.n + 3, NC)
                v.tensor_tensor(attn[:, :].rearrange("p (h d) -> p h d", d=HD), sums[:, :, 0:HD],
                                den[:, 1, :].rearrange("p (h u) -> p h u", u=1).broadcast_to([P, NH, HD]),
                                ALU.mult).then_inc(a_["at"], 1)

            def gated(m):
                wait(dve, a_["pj"], m.n + 1)
                wait(dve, s_out[m.p], 16 * m.pairs)
                wait(dve, s_modg, 16 * (m.b + 1))
                v.scalar_tensor_tensor(out=x1[:, m.p, :], in0=bank[2][:, 0:D], scalar=1.0 / WS,
                                       in1=mod_g[:, :], op0=ALU.mult, op1=ALU.mult).then_inc(a_["t1"], 1)

            def second_stats(m):
                wait(dve, a_["x1"], m.n + 1)
                stats(x1[:, m.p, :], 1, "st2")

            def second_centre(m):
                wait(dve, a_["mv2"], m.n + 1)
                wait(dve, a_["h2lo"], m.n)
                if m.c == 0:
                    wait(dve, s_modb, 16 * (m.b + 1))
                centred(x1[:, m.p, :], 1, h2[:, :], mod_b, "xc2")

            def weights_low(m, half, done):
                cols = slice(half * PIECE // 2, (half + 1) * PIECE // 2)
                wait(dve, a_["whi"], m.n + 1)
                carry(dve)
                v.scalar_tensor_tensor(out=piece(m, 1, half), in0=stage[:, m.p, cols], scalar=WS,
                                       in1=piece(m, 0, half), op0=ALU.mult, op1=ALU.subtract)\
                    .then_inc(a_[done], 1)

            steps_a(dve, steps_of(ORDER_DVE, {
                "stats": first_stats, "mv": lambda m: mean_var(m, 0, "st", "h", "mv"), "xc": first_centre,
                "h": first_modulated, "vlo": v_low, "rope": rope, "f": features, "sloq": q_low, "kTs": k_copy,
                "m0": lambda m: mask(m, 0), "m1": lambda m: mask(m, 1), "stl": state_low,
                "den": denominator, "at": quotient, "t1": gated, "stats2": second_stats,
                "mv2": lambda m: mean_var(m, 1, "st2", "h2", "mv2"), "xc2": second_centre,
                "h2": lambda m: modulated(m, 1, h2[:, :], mod_b, "xc2", "rs2", "h2"),
                "wlo": lambda m: weights_low(m, 0, "wlo"), "wlo2": lambda m: weights_low(m, 1, "wlo2")}))

            ec = [E, NC]
            def tile(k):
                return stage[:, :, :].rearrange("p q n -> p (q n)")[:, 256 * k:256 * (k + 1)]

            def full(k):
                return tile(k).rearrange("p (e i) -> p e i", e=E)

            def over_e(t):
                return t.rearrange("p e i -> p i e")

            def row(k):
                return small[:, k, :]

            def each_e(r):
                return r.rearrange("p (u i) -> p u i", u=1).broadcast_to([P] + ec)

            def each_i(r):
                return r.rearrange("p (e u) -> p e u", u=1).broadcast_to([P] + ec)

            top, rs, best, r1, r2, cw1, cw2 = (row(k) for k in range(7))
            m1, m2 = row(7), row(8)
            start, cnt, nblk, nblk_c, base = (small[:, k, 0:E] for k in range(9, 14))
            prob, shifted, oh1, oh2, eq, sel, tot, slots = (full(k) for k in range(8))
            lg = logits[:, :, :]

            dve.wait_ge(a_["lge"], NC)
            dve.wait_ge(a_["wlo2"], NC)
            link(v.tensor_reduce(top, over_e(lg), AX_X, ALU.max))
            link(v.tensor_tensor(shifted, lg, each_e(top), ALU.subtract))
            marks["shift"] = link.n
            dve.wait_ge(s_act, ACT_EXP2)
            link(v.tensor_reduce(rs, over_e(prob), AX_X, ALU.add))
            link(v.reciprocal(rs, rs))
            link(v.tensor_tensor(prob, prob, each_e(rs), ALU.mult))
            for oh, m_ in ((oh1, m1), (oh2, m2)):
                if oh is oh2:
                    link(v.scalar_tensor_tensor(out=tile(0), in0=tile(2), scalar=-2.0, in1=tile(0),
                                                op0=ALU.mult, op1=ALU.add))
                link(v.tensor_reduce(m_, over_e(prob), AX_X, ALU.max))
                link(v.tensor_tensor(eq, prob, each_e(m_), ALU.is_equal))
                link(v.tensor_tensor(eq, eq, each_i(rev[:, :]), ALU.mult))
                link(v.tensor_reduce(best, over_e(eq), AX_X, ALU.max))
                link(v.tensor_tensor(oh, eq, each_e(best), ALU.is_equal))
            link(v.tensor_tensor(tile(5)[:, 0:E * NC // 2].bitcast(F16).rearrange("p (e i) -> p e i", e=E),
                                 oh1, oh2, ALU.add))
            marks["sel"] = link.n
            link(v.scalar_tensor_tensor(out=rs, in0=m1, scalar=TOP_EPS, in1=m2, op0=ALU.add, op1=ALU.add))
            link(v.reciprocal(rs, rs))
            for cw, m_ in ((cw1, m1), (cw2, m2)):
                link(v.scalar_tensor_tensor(out=cw, in0=m_, scalar=1.0 / WS, in1=rs,
                                            op0=ALU.mult, op1=ALU.mult))
            link(v.memset(w_ones, 1.0))
            dve.wait_ge(s_pe, PE_RANK)
            cum = tile(4)
            link(v.tensor_copy(tile(6), bank[2][:, 0:E * NC]))
            link(v.tensor_tensor_scan(cum, w_ones, tile(6), 0.0, ALU.mult, ALU.add))
            link(v.tensor_tensor(tile(7), bank[1][:, 0:E * NC], cum, ALU.add))
            link(v.tensor_tensor(tile(7), tile(7), tile(6), ALU.subtract))
            cum_e = full(4)[:, :, NC - 1]
            link(v.memset(start, 0.0))
            link(v.tensor_copy(start[:, 1:E], cum_e[:, 0:E - 1]))
            link(v.tensor_tensor(cnt, cum_e, start, ALU.subtract))
            link(v.tensor_tensor(full(6), each_i(cnt), each_e(tile_f[:, :]), ALU.is_gt))
            link(v.tensor_reduce(nblk, full(6), AX_X, ALU.add))
            link(v.tensor_tensor_scan(nblk_c, w_ones[:, 0:E], nblk, 0.0, ALU.mult, ALU.add))
            link(v.tensor_tensor(base, nblk_c, nblk, ALU.subtract))
            link(v.scalar_tensor_tensor(out=base, in0=base, scalar=float(P), in1=start,
                                        op0=ALU.mult, op1=ALU.subtract))
            link(v.tensor_tensor(slots, slots, each_i(base), ALU.add))
            for k, oh in enumerate((oh1, oh2)):
                link(v.tensor_tensor(oh, oh, slots, ALU.mult))
                link(v.tensor_reduce(slot_f[:, 1, k, :], over_e(oh), AX_X, ALU.add))
            link(v.tensor_copy(slot_i[:, 1, :, :], slot_f[:, 1, :, :]))
            link(v.tensor_scalar(slot_i[:, 0, :, :], slot_i[:, 1, :, :], 7, None, ALU.logical_shift_right))
            link(v.tensor_scalar(slot_i[:, 1, :, :], slot_i[:, 1, :, :], P - 1, None, ALU.bitwise_and))
            link(v.tensor_copy(slot_f[:, :, :, :], slot_i[:, :, :, :]))
            marks["slot"] = link.n
            fits = xt[:, 0:TB * E].rearrange("p (j e) -> p j e", e=E)
            link(v.tensor_tensor(fits, nblk_c.rearrange("p (u e) -> p u e", u=1).broadcast_to([P, TB, E]),
                                 iota_f[:, 0:TB].rearrange("p (j u) -> p j u", u=1).broadcast_to([P, TB, E]),
                                 ALU.is_le))
            link(v.tensor_reduce(cwT[:, :], fits, AX_X, ALU.add))
            link(v.tensor_scalar(cwT[:, :], cwT[:, :], float(E - 1), None, ALU.min))
            eight = cwT.rearrange("p (g c) -> p g c", c=UC)
            digits = xt[:, 1024:1024 + TB // UC]
            link(v.tensor_copy(digits, eight[:, :, UC - 1]))
            for c in range(UC - 2, -1, -1):
                link(v.scalar_tensor_tensor(out=digits, in0=digits, scalar=float(E), in1=eight[:, :, c],
                                            op0=ALU.mult, op1=ALU.add))
            G = TB // UC
            link(v.tensor_copy(block_e[:, 0:G], digits))
            link(v.tensor_copy(block_e[:, G:2 * G - 1], eight[:, 0:-1, UC - 1]))
            link(v.tensor_scalar(block_e[:, G:2 * G - 1], block_e[:, G:2 * G - 1], 3 * UC, None,
                                 ALU.logical_shift_left))
            link(v.tensor_tensor(block_e[:, 1:G], block_e[:, 1:G], block_e[:, G:2 * G - 1], ALU.bitwise_or))
            marks["block_e"] = link.n

            def two_chunks(a):
                def slots_of(u, n):
                    return slot_f[:, u, :, bass.ds(2 * a.n, 2)].rearrange("p k (i u) -> p k i u", u=1)\
                        .broadcast_to([P, 2, 2, n])

                def numbers(n):
                    return iota_f[:, 0:n].rearrange("p (k i t) -> p k i t", k=1, i=1).broadcast_to([P, 2, 2, n])

                wait(dve, b_["rhs"], a.n - 1)
                v.tensor_tensor(b_block[:, a.p, :, :, :], numbers(TB), slots_of(0, TB), ALU.is_equal)\
                    .then_inc(b_["block"], 1)
                wait(dve, b_["mm"], a.n - 1)
                v.tensor_tensor(b_place[:, a.p, :, :, :], numbers(P), slots_of(1, P), ALU.is_equal)\
                    .then_inc(b_["place"], 1)

            steps_b(dve, two_chunks)
            dve.wait_ge(s_pe, PE_TABLE)
            table = bank[7][:, 0:2 * TB].rearrange("p (q j) -> p q j", q=2)
            pad, tok = b_rhs[:, 0, 0, 0, 0, :], b_rhs[:, 0, 0, 0, 1, :]
            link(v.tensor_copy(cwT[:, :], table[:, 1, :]))
            link(v.tensor_scalar(tok, table[:, 0, :], -1.0, None, ALU.add))
            link(v.tensor_scalar(pad, table[:, 0, :], 0.0, float(NOWHERE + 1), ALU.is_equal, ALU.mult))
            link(v.tensor_scalar(gidx[:, :], tok, 0.0, None, ALU.max))
            link(v.tensor_tensor(sidx[:, :], tok, pad, ALU.add))

            def load_gi(m):
                q, used = m.slot(GB)
                wait(dve, s_g[q], 16 * used)
                v.tensor_copy(gi[:, q:q + 1], gidx[:, bass.ds(m.n, 1)]).then_inc(c_["gi"], 1)

            for c in range(3):
                load_gi(At(0, c, UC))
            dve.wait_ge(c_["xT"], 1)
            v.tensor_copy(x16[:, 0, :], bank[0][:, 0:D].bitcast(F16)).then_inc(c_["xTe"], 1)

            def step_c(a):
                m = a.back(2)
                if m.inside(MAXB):
                    wait(dve, s_sc, 16 * (m.n - 1))
                    q = m.c % GB
                    v.tensor_copy(si[:, q:q + 1], sidx[:, bass.ds(m.n, 1)])
                    wait(dve, c_["y"], m.n + 1)
                    v.scalar_tensor_tensor(out=yw[:, m.p, :], in0=bank[1 + m.p][:, 0:D],
                                           scalar=cwT[:, bass.ds(m.n, 1)], in1=xg[:, q, D:2 * D],
                                           op0=ALU.mult, op1=ALU.mult).then_inc(c_["yw"], 1)
                m = a.back(-3)
                if m.inside(MAXB):
                    load_gi(m)
                m = a.back(-1)
                if m.inside(MAXB):
                    wait(dve, c_["xT"], m.n + 1)
                    wait(dve, c_["hB"], m.n - 1)
                    v.tensor_copy(x16[:, m.p, :], bank[7 * m.p][:, 0:D].bitcast(F16)).then_inc(c_["xTe"], 1)
                if a.inside(MAXB):
                    for g, ready, done in ((0, "gA", "glA"), (1, "gB", "glB")):
                        wait(dve, c_[ready], a.n + 1)
                        wait(dve, c_["y"], a.n - 1)
                        h_ = slice(g * 512, g * 512 + 512)
                        v.tensor_tensor(glo[:, a.p, h_], g32[:, a.p, h_], ghi[:, a.p, h_], ALU.subtract)\
                            .then_inc(c_[done], 1)

            steps_c(dve, step_c)

        @block.gpsimd
        def _(pool):
            link = Chain(pool, s_pool)
            g = nc.gpsimd
            for t in (ones, before, causal):
                link(g.memset(t[:, :], 1.0))
            link(g.memset(ident16[:, :], 0.0))
            link(g.memset(ident[:, :], 0.0))
            link(g.memset(eps[:, :], LN_EPS))
            link(g.memset(minus_half[:, :], -0.5))
            link(g.memset(v16[:, :, 0, :, HD:VW], 1.0))
            link(g.memset(v16[:, :, 1, :, HD:VW], 0.0))
            link(g.memset(state[:, :, :, :], 0.0))
            for t in (ident, ident16):
                link(g.affine_select(out=t[:, :], in_=t[:, :], compare_op=ALU.not_equal, fill=1.0, base=0,
                                     pattern=[[-1, P]], channel_multiplier=1))
            for t, base in ((causal, 0), (before, -1)):
                link(g.affine_select(out=t[:, :], in_=t[:, :], compare_op=ALU.is_ge, fill=0.0, base=base,
                                     pattern=[[1, P]], channel_multiplier=-1))
            link(g.iota(iota_i[:, :], pattern=[[1, P]], base=0, channel_multiplier=0))
            link(g.tensor_copy(iota_f[:, :], iota_i[:, :]))
            assert link.n == POOL_CONST, link.n
            link(g.iota(tile_i[:, :], pattern=[[P, NC]], base=0, channel_multiplier=0))
            link(g.tensor_copy(tile_f[:, :], tile_i[:, :]))
            link(g.iota(tile_i[:, :], pattern=[[P, NC]], base=1, channel_multiplier=1))
            link(g.tensor_copy(id1[:, :], tile_i[:, :]))
            link(g.iota(iota_i[:, 0:E], pattern=[[-1, E]], base=E, channel_multiplier=0))
            link(g.tensor_copy(rev[:, :], iota_i[:, 0:E]))

            def root(k, ready, mid, done, count):
                wait(pool, ready, count)
                g.tensor_tensor(var[:, k:k + 1], mv[:, k, 1:2], eps[:, :], ALU.add).then_inc(mid, 1)
                wait(pool, mid, count)
                g.tensor_tensor(rstd[:, k:k + 1], var[:, k:k + 1], minus_half[:, :], ALU.pow)\
                    .then_inc(done, 1)

            def scores_low(m, group):
                wait(pool, a_[f"mh{group}"], m.n + 1)
                wait(pool, a_[f"pv{group}"], m.n)
                g.tensor_tensor(amlo[:, group, :, :], am[:, group, :, :], amhi[:, group, :, :], ALU.subtract)\
                    .then_inc(a_[f"ml{group}"], 1)

            def first_root(m):
                wait(pool, a_["h"], m.n)
                root(0, a_["mv"], a_["ve"], a_["rs"], m.n + 1)

            def second_root(m):
                wait(pool, a_["h2"], m.n)
                root(1, a_["mv2"], a_["ve2"], a_["rs2"], m.n + 1)

            def low(dst, src, high, done):
                g.tensor_tensor(dst, src, high, ALU.subtract).then_inc(a_[done], 1)

            def attention_low(m):
                wait(pool, a_["ahi"], m.n + 1)
                wait(pool, a_["aT"], m.n)
                low(a16[:, 1, :], attn[:, :], a16[:, 0, :], "alo")

            def h_low(m):
                wait(pool, a_["hhi"], m.n + 1)
                wait(pool, a_["hT"], m.n)
                low(h16[:, 1, :], h[:, :], h16[:, 0, :], "hlo")

            def h2_low(m):
                wait(pool, a_["h2hi"], m.n + 1)
                low(h2_16[:, m.p, 1, :], h2[:, :], h2_16[:, m.p, 0, :], "h2lo")

            def k_low(m):
                wait(pool, a_["shi"], m.n + 1)
                f = feat[:, D:2 * D].rearrange("p (h u d) -> p h u d", h=NH, u=1)
                low(kst[:, :, 2:4, :], f.broadcast_to([P, NH, 2, HD]), kst[:, :, 0:2, :], "slok")

            def residual(m):
                wait(pool, a_["t1"], m.n + 1)
                g.tensor_tensor(x1[:, m.p, :], x1[:, m.p, :], x_slot(m), ALU.add).then_inc(a_["x1"], 1)

            def rotated(m):
                wait(pool, a_["rope"], m.n + 1)
                g.tensor_tensor(ra[:, :], ra[:, :], rb[:, :], ALU.add).then_inc(a_["R"], 1)

            steps_a(pool, steps_of(ORDER_POOL, {
                "rs": first_root, "hlo": h_low, "slok": k_low, "R": rotated, "ml0": lambda m: scores_low(m, 0),
                "ml1": lambda m: scores_low(m, 1), "alo": attention_low, "x1": residual, "rs2": second_root,
                "h2lo": h2_low}))

            pool.wait_ge(s_dve, marks["block_e"])

            def two_chunks(a):
                i = bass.ds(2 * a.n, 2)
                wait(pool, b_["block"], a.n + 1)
                wait(pool, b_["mm"], a.n - 1)
                for q, val in enumerate((id1[:, i].rearrange("p (k i) -> p k i", k=1).broadcast_to([P, 2, 2]),
                                         small[:, 5:7, i])):
                    last = g.tensor_tensor(b_rhs[:, a.p, :, :, q, :], b_block[:, a.p, :, :, :],
                                           val.rearrange("p k (i u) -> p k i u", u=1).broadcast_to([P, 2, 2, TB]),
                                           ALU.mult)
                last.then_inc(b_["rhs"], 1)

            steps_b(pool, two_chunks)

            pool.wait_ge(s_row[0], 16 * (NC // 2))
            pool.wait_ge(s_row[1], 16 * (NC // 2))
            pool.wait_ge(s_gb, 16)
            pool.wait_ge(s_out[0], 16 * (NC // 2))
            pool.wait_ge(s_out[1], 16 * (NC // 2))

            def gather(m):
                wait(pool, c_["gi"], m.n + 1)
                wait(pool, c_["yw"], m.n - 3)
                carry(pool)
                q = m.c % GB
                g.indirect_dma_start(xg[:, q, :], None, rows_d,
                                     bass.IndirectOffsetOnAxis(ap=gi[:, q:q + 1], axis=0)).then_inc(s_g[q], 16)

            gather(At(0, 0, UC))
            gather(At(0, 1, UC))

            def step_c(a):
                m = a.back(2)
                if m.inside(MAXB):
                    wait(pool, c_["yw"], m.n + 1)
                    wait(pool, s_sc, 16 * m.n)
                    carry(pool)
                    g.indirect_dma_start(out_rows, bass.IndirectOffsetOnAxis(ap=si[:, m.c % GB:m.c % GB + 1], axis=0),
                                         yw[:, m.p, :], None, bounds_check=T - 1, oob_is_err=False,
                                         compute_op=ALU.add).then_inc(s_sc, 16)
                m = a.back(-2)
                if m.inside(MAXB):
                    gather(m)

            steps_c(pool, step_c)
            pool.wait_ge(s_sc, 16 * MAXB)

        @block.scalar
        def _(act):
            v = nc.scalar

            def copy(out_, in_, scale=1.0):
                return v.activation(out_, in_, ACT.Copy, scale=scale)

            act.wait_ge(s_ld["c"], 16)
            v.activation(c_exp, c_raw, ACT.Exp, scale=-1.0).then_inc(s_act, 1)
            act.wait_ge(s_ld["wq"], 16)
            copy(wqhi[:, :, :], wq_raw, WS).then_inc(s_act, 1)
            act.wait_ge(s_ld["wo"], 16)
            copy(wohi[:, :, :], wo_raw, WS).then_inc(s_act, 1)
            act.wait_ge(s_pool, POOL_CONST)

            def parts(t):
                return t.bitcast(F16).rearrange("p (q n) -> p q n", q=2)

            def earlier_done(m):
                prev = m.back(1)
                if prev.inside(NC) and prev.c > 0:
                    wait(act, a_["ear"], (CPB - 1) * prev.b + prev.c)

            def h_high(m):
                wait(act, a_["h"], m.n + 1)
                wait(act, a_["hT"], m.n)
                copy(h16[:, 0, :], h[:, :]).then_inc(a_["hhi"], 1)

            def h_copy(m):
                wait(act, a_["hT"], m.n + 1)
                wait(act, a_["v"], m.n)
                copy(hT[:, :, :], parts(bank[0][:, 0:D])).then_inc(a_["hTe"], 1)

            def v_high(m):
                wait(act, a_["v"], m.n + 1)
                wait(act, a_["pv1"], m.n - CPB + 1)
                copy(v16[:, m.c, 0, :, 0:HD], bank[2][:, 0:D].rearrange("p (h d) -> p h d", d=HD), 1.0 / WS)\
                    .then_inc(a_["vhi"], 1)

            def relu_exp(m):
                wait(act, a_["R"], m.n + 1)
                wait(act, a_["sloq"], m.n)
                wait(act, a_["slok"], m.n)
                v.activation(rb[:, :], ra[:, :], ACT.Relu)
                v.activation(feat[:, :], ra[:, :], ACT.Exp).then_inc(a_["exp"], 1)

            def stack_high(m):
                wait(act, a_["f"], m.n + 1)
                wait(act, a_["Tk"], m.n)
                prev = m.back(1)
                if prev.inside(NC) and prev.c < CPB - 1:
                    wait(act, a_["state"], (CPB - 1) * prev.b + prev.c + 1)
                f = feat[:, :].rearrange("p (q h u d) -> p q h u d", q=2, h=NH, u=1)
                copy(qst[:, :, 0:3:2, :], f[:, 0].broadcast_to([P, NH, 2, HD]))
                copy(kst[:, :, 0:2, :], f[:, 1].broadcast_to([P, NH, 2, HD])).then_inc(a_["shi"], 1)

            def q_copy(m):
                wait(act, a_["Tq"], m.n + 1)
                wait(act, a_["sc1"], m.n)
                earlier_done(m)
                copy(qstT[:, :], bank[3][:, :].bitcast(F16)).then_inc(a_["qTs"], 1)

            def scores_high(m, g):
                wait(act, a_[f"m{g}"], m.n + 1)
                wait(act, a_[f"pv{g}"], m.n)
                copy(amhi[:, g, :, :], am[:, g, :, :]).then_inc(a_[f"mh{g}"], 1)

            def state_high(m):
                if m.c == CPB - 1:
                    return
                wait(act, a_["state"], (CPB - 1) * m.b + m.c + 1)
                earlier_done(m)
                copy(own(state[:, m.p, 0, :], 0), own(bank[4][:, 0:NH * VW], 0))
                copy(own(state[:, m.p, 0, :], 1), own(bank[4][:, 0:NH * VW], 1)).then_inc(a_["sth"], 1)

            def attention_high(m):
                wait(act, a_["at"], m.n + 1)
                wait(act, a_["aT"], m.n)
                copy(a16[:, 0, :], attn[:, :]).then_inc(a_["ahi"], 1)

            def attention_copy(m):
                wait(act, a_["aT"], m.n + 1)
                wait(act, a_["pj"], m.n)
                copy(aT[:, :, :], parts(bank[0][:, 0:D])).then_inc(a_["aTe"], 1)

            def h2_high(m):
                wait(act, a_["h2"], m.n + 1)
                wait(act, s_row[m.p], 16 * m.pairs)
                wait(act, a_["h2T"], m.n - 1)
                copy(h2_16[:, m.p, 0, :], h2[:, :]).then_inc(a_["h2hi"], 1)

            def h2_copy(m):
                wait(act, a_["h2T"], m.n + 1)
                wait(act, a_["lg"], m.n)
                copy(h2T[:, :, :], parts(bank[0][:, 0:D])).then_inc(a_["h2Te"], 1)

            def logits_out(m):
                wait(act, a_["lg"], m.n + 1)
                copy(logits[:, :, bass.ds(m.n, 1)], bank[0][:, 0:E].rearrange("p (e u) -> p e u", u=1), 1.0 / WS)\
                    .then_inc(a_["lge"], 1)

            def weights_high(m):
                wait(act, s_w[m.p], 16 * (m.pairs + 1))
                copy(piece(m, 0), stage[:, m.p, :], WS).then_inc(a_["whi"], 1)

            steps_a(act, steps_of(ORDER_ACT, {
                "hhi": h_high, "hTe": h_copy, "vhi": v_high, "exp": relu_exp, "shi": stack_high, "qTs": q_copy,
                "mh0": lambda m: scores_high(m, 0), "mh1": lambda m: scores_high(m, 1), "sth": state_high,
                "ahi": attention_high, "aTe": attention_copy, "h2hi": h2_high, "h2Te": h2_copy,
                "lge": logits_out, "whi": weights_high}))

            act.wait_ge(s_dve, marks["shift"])
            flat = stage[:, :, :].rearrange("p q n -> p (q n)")
            v.activation(flat[:, 0:256], flat[:, 256:512], ACT.Exp).then_inc(s_act, 1)

            def step_c(a):
                if a.inside(MAXB):
                    for g, ready, done, freed in ((0, "hA", "gA", "glA"), (1, "hB", "gB", "glB")):
                        src = bank[3 + 2 * a.p + g][:, :]
                        h_ = slice(g * 512, g * 512 + 512)
                        wait(act, c_[ready], a.n + 1)
                        wait(act, c_[freed], a.n - 1)
                        v.activation(g32[:, a.p, h_], src, ACT.Gelu, scale=1.0 / WS)
                        wait(act, c_["y"], a.n - 1)
                        v.activation(ghi[:, a.p, h_], src, ACT.Gelu, scale=1.0 / WS).then_inc(c_[done], 1)

            steps_c(act, step_c)

        @block.tensor
        def _(pe):
            t = nc.tensor

            def mm3(dst, xhi_, xlo_, whi, wlo, start=True, stop=True):
                t.matmul(dst, xhi_, whi, start=start, stop=False)
                t.matmul(dst, xhi_, wlo, start=False, stop=False)
                return t.matmul(dst, xlo_, whi, start=False, stop=stop)

            pe.wait_ge(s_pool, POOL_CONST)
            pe.wait_ge(s_dve, marks["silu"])
            pe.wait_ge(s_ld["rw"], 16)
            for i, src in enumerate((c_silu, rw_raw)):
                for k in range(KT):
                    o = (i * KT + k) * B
                    last = t.transpose(bank[0][:, o:o + B], src[:, k * P:(k + 1) * P], ident[0:B, 0:B])
            last.then_inc(s_pe, 1)
            pe.wait_ge(s_dve, marks["t"])
            pe.wait_ge(s_ld["wmod"], 16)
            for j in range(3):
                for k in range(KT):
                    last = t.matmul(bank[MOD_BANK[j]][0:B, :], cT[:, k, :], wmod_raw[:, k, 512 * j:512 * j + 512],
                                    start=(k == 0), stop=(k == KT - 1))
                if j != 1:
                    last.then_inc(s_pe, 1)
            pe.wait_ge(s_dve, marks["wo"])

            def scores(m, g):
                if g == 0:
                    wait(pe, a_["qTs"], m.n + 1)
                    wait(pe, a_["kTs"], m.n + 1)
                    wait(pe, a_["m1"], m.n)
                else:
                    wait(pe, a_["m0"], m.n + 1)
                for h_ in range(HG * g, HG * g + HG):
                    j, odd = h_ // 2, h_ % 2
                    rows = slice(64 * odd, 64 * odd + 64)
                    cols = slice(j * P, j * P + P)
                    o = (j % 4) * P
                    last = t.matmul(bank[5 + odd][:, o:o + P], kstT[rows, cols], qstT[rows, cols],
                                    start=True, stop=True)
                last.then_inc(a_[f"sc{g}"], 1)

            def earlier(m):
                if m.c == 0:
                    return
                wait(pe, a_["at"], m.n)
                wait(pe, a_["stl"], (CPB - 1) * m.b + m.c)
                for j in range(NH // 2):
                    two = slice(2 * j * VW, (2 * j + 2) * VW)
                    for i in range(2):
                        last = t.matmul(bank[7][:, two], qstT[:, j * P:(j + 1) * P], state[:, 1 - m.p, i, two],
                                        start=(j == i == 0), stop=False, skip_group_check=True)
                last.then_inc(a_["ear"], 1)

            def attend(m, g):
                wait(pe, a_[f"ml{g}"], m.n + 1)
                if g == 0:
                    wait(pe, a_["at"], m.n)
                for h_ in range(HG * g, HG * g + HG):
                    o = bank[7][:, h_ * VW:(h_ + 1) * VW]
                    q = slice(h_ // 2 % 4 * P, (h_ // 2 % 4 + 1) * P)
                    hi, lo = amhi[:, g, h_ % 2, q], amlo[:, g, h_ % 2, q]
                    vhi, vlo = v16[:, m.c, 0, h_, :], v16[:, m.c, 1, h_, :]
                    t.matmul(o, hi, vhi, start=(m.c == 0), stop=False, skip_group_check=True)
                    t.matmul(o, hi, vlo, start=False, stop=False, skip_group_check=True)
                    last = t.matmul(o, lo, vhi, start=False, stop=True, skip_group_check=True)
                last.then_inc(a_[f"pv{g}"], 1)

            def transpose_parts(dst, src, n=2 * KT):
                for j in range(n):
                    last = t.transpose(dst[:, :].bitcast(F16)[:, j * P:(j + 1) * P], src[:, j * P:(j + 1) * P],
                                       ident16[:, :])
                return last

            def flat3(t_):
                return t_.rearrange("p q n -> p (q n)")

            def flat4(t_):
                return t_.rearrange("p h c d -> p (h c d)")

            def product(dst, xT_, whi, wlo, n):
                for k in range(KT):
                    c_k = slice(k * P, (k + 1) * P)
                    last = mm3(dst, xT_[:, 0, c_k], xT_[:, 1, c_k], whi[:, k, n], wlo[:, k, n],
                               start=(k == 0), stop=(k == KT - 1))
                return last

            def bank_free(m, *users):
                for name, after in users:
                    u = m.back(-after)
                    if u.inside(NC):
                        wait(pe, a_[name], u.n + 1)
                        return

            def h_transpose(m):
                wait(pe, a_["hlo"], m.n + 1)
                bank_free(m, ("h2Te", -5), ("aTe", -4), ("hTe", -1))
                transpose_parts(bank[0], flat3(h16[:, :, :])).then_inc(a_["hT"], 1)

            def v_product(m):
                bank_free(m, ("t1", -4), ("vlo", -1))
                product(bank[2][:, 0:D], hT, wqhi, wqlo, slice(2 * D, 3 * D)).then_inc(a_["v"], 1)

            def qk_product(m):
                wait(pe, a_["hTe"], m.n + 1)
                wait(pe, a_["rope"], m.n)
                product(bank[1][:, :], hT, wqhi, wqlo, slice(0, 2 * D)).then_inc(a_["qk"], 1)

            def q_transpose(m):
                wait(pe, a_["sloq"], m.n + 1)
                wait(pe, a_["qTs"], m.n)
                transpose_parts(bank[3], flat4(qst[:, :, :, :]), 8).then_inc(a_["Tq"], 1)

            def k_transpose(m):
                wait(pe, a_["slok"], m.n + 1)
                wait(pe, a_["m1"], m.n)
                transpose_parts(bank[6], flat4(kst[:, :, :, :]), 8).then_inc(a_["Tk"], 1)

            def state_product(m):
                if m.c == CPB - 1:
                    return
                wait(pe, a_["slok"], m.n + 1)
                wait(pe, a_["vlo"], m.n + 1)
                wait(pe, a_["stl"], (CPB - 1) * m.b + m.c)
                for j in range(NH // 2):
                    two = slice(2 * j, 2 * j + 2)
                    o = bank[4][:, two.start * VW:two.stop * VW]
                    k_ = kst[:, two, :, :].rearrange("p h c d -> p (h c d)")
                    for i in range(2):
                        last = t.matmul(o, k_, v16[:, m.c, i, two, :].rearrange("p h w -> p (h w)"),
                                        start=(m.c == j == i == 0), stop=(i == 1), skip_group_check=True)
                last.then_inc(a_["state"], 1)

            def a_transpose(m):
                wait(pe, a_["alo"], m.n + 1)
                bank_free(m, ("hTe", 3), ("h2Te", -2), ("aTe", -1))
                transpose_parts(bank[0], flat3(a16[:, :, :])).then_inc(a_["aT"], 1)

            def projection(m):
                wait(pe, a_["aTe"], m.n + 1)
                bank_free(m, ("vlo", 3), ("t1", -1))
                product(bank[2][:, 0:D], aT, wohi, wolo, slice(0, D)).then_inc(a_["pj"], 1)

            def h2_transpose(m):
                wait(pe, a_["h2lo"], m.n + 1)
                bank_free(m, ("lge", -1), ("aTe", 1))
                transpose_parts(bank[0], flat3(h2_16[:, m.p, :, :])).then_inc(a_["h2T"], 1)

            def router(m):
                wait(pe, a_["h2Te"], m.n + 1)
                bank_free(m, ("aTe", 2))
                product(bank[0][:, 0:E], h2T, rwhi, rwlo, slice(0, E)).then_inc(a_["lg"], 1)

            steps_a(pe, steps_of(ORDER_PE, {
                "hT": h_transpose, "v": v_product, "qk": qk_product, "Tq": q_transpose, "Tk": k_transpose,
                "state": state_product, "sc0": lambda m: scores(m, 0), "sc1": lambda m: scores(m, 1),
                "earlier": earlier, "pv0": lambda m: attend(m, 0), "pv1": lambda m: attend(m, 1),
                "aT": a_transpose, "pj": projection, "h2T": h2_transpose, "lg": router}))

            flat = stage[:, :, :].rearrange("p q n -> p (q n)")
            sel = flat[:, 5 * 256:5 * 256 + 128].bitcast(F16)
            pe.wait_ge(s_dve, marks["sel"])
            t.matmul(bank[1][:, 0:E * NC], before[:, :], sel, start=True, stop=True)
            t.matmul(bank[2][:, 0:E * NC], ones[:, :], sel, start=True, stop=True).then_inc(s_pe, 1)

            def two_chunks(a):
                wait(pe, b_["place"], a.n + 1)
                wait(pe, b_["rhs"], a.n + 1)
                for j in range(4):
                    k, i = j // 2, j % 2
                    last = t.matmul(bank[7][:, 0:2 * TB], b_place[:, a.p, k, i, :],
                                    b_rhs[:, a.p, k, i, :, :].rearrange("p q j -> p (q j)"),
                                    start=(isinstance(a.n, int) and a.n == j == 0),
                                    stop=(isinstance(a.n, int) and a.n == NC // 2 - 1 and j == 3))
                last.then_inc(b_["mm"], 1)

            steps_b(pe, two_chunks)
            pe.wait_ge(b_["mm"], NC // 2)
            pe.sem_inc(s_pe, 1)

            def xT(m):
                q, used = m.slot(GB)
                wait(pe, s_g[q], 16 * (used + 1))
                wait(pe, c_["xTe"], m.n - 1)
                transpose_parts(bank[7 * m.p], xg[:, q, 0:D].bitcast(F16)).then_inc(c_["xT"], 1)

            pe.wait_ge(s_dve, marks["block_e"])
            pe.wait_ge(a_["whi"], NC)
            pe.wait_ge(a_["wlo2"], NC)
            xT(At(0, 0, UC))

            expert = {}

            def step_c(a):
                if a.c == 0 and a.inside(MAXB):
                    digits = pe.value_load(block_e[0:1, bass.ds(a.b, 1)], min_val=0, max_val=E ** (UC + 1) - 1)
                    for c in (*range(UC), -1):
                        expert[c] = digits % E
                        digits = digits // E
                if a.back(-1).inside(MAXB):
                    xT(a.back(-1))
                if a.inside(MAXB):
                    e = expert[a.c]
                    wait(pe, c_["xTe"], a.n + 1)
                    for mt in range(MT):
                        g, q = mt // 4, mt % 4
                        if q == 0:
                            wait(pe, c_["gA" if g == 0 else "gB"], a.n - 1)
                        dst = bank[3 + 2 * a.p + g][:, q * P:(q + 1) * P]
                        for k in range(KT):
                            w_ = bass.ds(e * EW + (k * H + mt * P), P)
                            c_k = slice(k * P, (k + 1) * P)
                            last = mm3w(dst, w1hi[:, w_], w1lo[:, w_], x16[:, a.p, c_k], x16[:, a.p, D:2 * D][:, c_k],
                                        start=(k == 0), stop=(k == KT - 1))
                        if q == 3:
                            last.then_inc(c_["hA" if g == 0 else "hB"], 1)
                m = a.back(1)
                if m.inside(MAXB):
                    e = expert[a.c - 1]
                    wait(pe, c_["yw"], m.n - 1)
                    for mt in range(MT):
                        if mt % 4 == 0:
                            wait(pe, c_["glA" if mt == 0 else "glB"], m.n + 1)
                        w_ = bass.ds(e * EW + mt * D, D)
                        c_m = slice(mt * P, (mt + 1) * P)
                        last = mm3(bank[1 + m.p][:, 0:D], ghi[:, m.p, c_m], glo[:, m.p, c_m], w2hi[:, w_], w2lo[:, w_],
                                   start=(mt == 0), stop=(mt == MT - 1))
                    last.then_inc(c_["y"], 1)

            def mm3w(dst, whi, wlo, xhi_, xlo_, start, stop):
                t.matmul(dst, whi, xhi_, start=start, stop=False)
                t.matmul(dst, whi, xlo_, start=False, stop=False)
                return t.matmul(dst, wlo, xhi_, start=False, stop=stop)

            steps_c(pe, step_c)

        @block.sync
        def _(sp):
            def load_x(a):
                wait(sp, a_["h"], a.n - CPB + 1)
                carry(sp)
                sp.dma_start(x_slot(a), x_rows[bass.ds(a.n * P, P), :]).then_inc(s_x[a.c], 16)

            def load_mod(dst, b, lo, done):
                sp.dma_start(dst[:, :], mod_d[bass.ds(b, 1), lo * D:lo * D + dst.shape[1]].broadcast_to(
                    [P, dst.shape[1]])).then_inc(done, 16)

            def load_piece(a):
                wait(sp, a_["wlo2"], a.n - 1)
                if a.c < KT:
                    src = w1_v[:, bass.ds(a.b, 1), a.c, :].rearrange("p e h -> p (e h)")
                    dst = stage[:, a.p, :]
                else:
                    q = MT // 2
                    src = w2_v[:, bass.ds(a.b, 1), (a.c - KT) * q:(a.c - KT + 1) * q, :].rearrange(
                        "p e m d -> p (e m) d")
                    dst = stage[:, a.p, :].rearrange("p (m d) -> p m d", m=q)
                carry(sp)
                sp.dma_start(dst, src).then_inc(s_w[a.p], 16)

            sp.dma_start(c_raw, c_in).then_inc(s_ld["c"], 16)
            sp.dma_start(wmod_raw, wmod.rearrange("(k p) n -> p k n", p=P)).then_inc(s_ld["wmod"], 16)
            sp.dma_start(rw_raw, router_w).then_inc(s_ld["rw"], 16)
            load_x(At(0, 0, CPB))
            load_x(At(0, 1, CPB))
            sp.dma_start(wq_raw, w_qkv.rearrange("(k p) n -> p k n", p=P)).then_inc(s_ld["wq"], 16)
            sp.dma_start(cos_t[:, :, :], rope_cos).then_inc(s_ld["cos"], 16)
            sp.dma_start(sin_t[:, :, :, :], rope_sin).then_inc(s_ld["sin"], 16)
            sp.dma_start(wo_raw, w_out.rearrange("(k p) n -> p k n", p=P)).then_inc(s_ld["wo"], 16)
            sp.wait_ge(s_dve, marks["mod_a"])
            sp.dma_start(mod_d[:, 0:2 * D], mod_s[:, 0:2 * D]).then_inc(s_ms, 16)
            sp.wait_ge(s_ms, 16)
            load_mod(mod_a, 0, 0, s_moda)
            load_piece(At(0, 0, CPB))

            def rest_of_modulation():
                sp.wait_ge(s_dve, marks["mod"])
                sp.dma_start(mod_d[:, 2 * D:6 * D], mod_s[:, 2 * D:6 * D]).then_inc(s_ms, 16)
                sp.wait_ge(s_ms, 32)
                load_mod(mod_g, 0, 2, s_modg)
                load_mod(mod_b, 0, 3, s_modb)
                sp.dma_start(rows_d.rearrange("(b s) n -> b s n", b=B)[:, :, D:2 * D],
                             mod_d[:, MOD["gb"]:MOD["gb"] + D].rearrange("b (u d) -> b u d", u=1)
                             .broadcast_to([B, S, D])).then_inc(s_gb, 16)

            def step(a):
                m = a.back(4)
                ends = m.c == CPB - 1 and m.back(-1).inside(NC)
                if a.back(-2).inside(NC):
                    load_x(a.back(-2))
                if m.inside(NC):
                    wait(sp, a_["x1"], m.n + 1)
                    carry(sp)
                    sp.dma_start(out_rows[bass.ds(m.n * P, P), :], x1[:, m.p, :]).then_inc(s_out[m.p], 16)
                    if ends:
                        load_mod(mod_g, m.b + 1, 2, s_modg)
                if a.c == CPB - 1 and a.back(-1).inside(NC):
                    wait(sp, a_["h"], a.n + 1)
                    carry(sp)
                    load_mod(mod_a, a.b + 1, 0, s_moda)
                if a.back(-1).inside(NC):
                    load_piece(a.back(-1))
                if m.inside(NC):
                    if ends:
                        wait(sp, a_["h2"], m.n + 1)
                        carry(sp)
                        load_mod(mod_b, m.b + 1, 3, s_modb)
                    wait(sp, a_["h2lo"], m.n + 1)
                    carry(sp)
                    sp.dma_start(rows_d[bass.ds(m.n * P, P), 0:D],
                                 h2_16[:, m.p, :, :].rearrange("p q n -> p (q n)").bitcast(F32))\
                        .then_inc(s_row[m.p], 16)

            steps_a(sp, step, rest_of_modulation)


_INS = ["L0_attn_x", "L0_attn_w_qkv", "L0_attn_w_out", "L0_ffn_router_w", "L0_ffn_w1", "L0_ffn_w2",
        "L0_c", "L0_wmod"]


def rope_tables():
    hd2 = HD // 2
    inv = (np.float32(1.0) / np.float32(10000.0) ** (np.arange(hd2, dtype=np.float32) / np.float32(hd2)))
    ang = np.arange(S, dtype=np.float32)[:, None] * inv.astype(np.float32)[None, :]
    scale = np.float32(Q_SCALE / WS)
    cos, sin = np.cos(ang) * scale, np.sin(ang) * scale
    by_place = lambda t: np.ascontiguousarray(
        t.reshape((CPB, P) + t.shape[1:]).swapaxes(0, 1), dtype=np.float32)
    return by_place(cos), by_place(np.stack([-sin, sin], axis=1))


def kernel(**inputs):
    import concourse.bacc as _bacc
    from concourse.bass_utils import run_bass_kernel_spmd as _run

    nc = _bacc.Bacc("TRN2", target_bir_lowering=False, num_devices=1)
    arrays = {f"in_{name}_dram": np.ascontiguousarray(inputs[name]) for name in _INS}
    arrays["rope_cos"], arrays["rope_sin"] = rope_tables()
    args = [nc.dram_tensor(name, a.shape, mybir.dt.from_np(a.dtype), kind="ExternalInput").ap()
            for name, a in arrays.items()]
    args.append(nc.dram_tensor("out_dram", (B, S, D), F32, kind="ExternalOutput").ap())
    adaln_block(nc, *args)
    r = _run(nc, [arrays], core_ids=[0])
    return r.results[0]["out_dram"]
```
